# Optimizing a Trainium2 kernel written in Bass

```python
import numpy as np
import jax
import jax.numpy as jnp

def _softmax(x, axis=-1):
    return jax.nn.softmax(x, axis=axis)

def _gelu(x):
    return jax.nn.gelu(x, approximate=True)

def _silu(x):
    return jax.nn.silu(x)

def _sigmoid(x):
    return jax.nn.sigmoid(x)

def _layernorm(x, axis=-1, eps=1e-05):
    m = jnp.mean(x, axis=axis, keepdims=True)
    v = jnp.var(x, axis=axis, keepdims=True)
    return (x - m) / jnp.sqrt(v + eps)

def _scatter_add(tgt, idx, src, axis=0):
    return tgt.at[idx].add(src)

def _segment_sum(src, seg, n):
    return jax.ops.segment_sum(src, seg, n)
kernel_name = 'mk_rec_standalone_d1_rec_r8_666160'

def setup_inputs(seed: int=0):
    np.random.seed(seed)
    _w = jnp.asarray

    def _rec_inputs():
        import jax
        import jax.numpy as jnp
        _rk = jax.random.key(seed)
        r_x_ids = jax.random.randint(jax.random.fold_in(_rk, 1), (12500,), 0, 12500, jnp.int32)
        return r_x_ids
    r_x_ids = _rec_inputs()

    def _L0_rec_setup():
        import jax, jax.numpy as jnp
        import numpy as np
        N = 12500
        E = 400000
        D = 128
        NEG_SLOPE = 0.2

        def _spmm(row, col, vals, x):
            msg = vals[:, None] * x[col]
            return jax.ops.segment_sum(msg, row, num_segments=N)

        def _layer(x_prev, row, col, vals, W_a, b_a, W_b, b_b):
            h = _spmm(row, col, vals, x_prev)
            z = (h + x_prev) @ W_a.T + b_a + h * x_prev @ W_b.T + b_b
            return jnp.where(z >= 0, z, NEG_SLOPE * z)
        key = jax.random.key(seed)
        ks = jax.random.split(key, 16)
        x_ids = jnp.arange(N, dtype=jnp.int64) if jax.config.jax_enable_x64 else jnp.arange(N, dtype=jnp.int32)
        row = jax.random.randint(ks[0], (E,), 0, N)
        col = jax.random.randint(ks[1], (E,), 0, N)
        vals = jax.random.uniform(ks[2], (E,), dtype=jnp.float32)

        def xavier(k, shape):
            fan_in, fan_out = (shape[1], shape[0])
            limit = float(np.sqrt(6.0 / (fan_in + fan_out)))
            return jax.random.uniform(k, shape, jnp.float32, -limit, limit)
        emb = xavier(ks[3], (N, D))
        inp = {'x_ids': x_ids, 'row': row, 'col': col, 'vals': vals, 'emb': emb}
        names = ['W1_1', 'W1_2', 'W2_1', 'W2_2', 'W3_1', 'W3_2']
        for i, nm in enumerate(names):
            inp[nm] = xavier(ks[4 + i], (D, D))
            inp['b' + nm[1:]] = jnp.zeros((D,), jnp.float32)
        return inp
    _L0_rec_all = _L0_rec_setup()
    _L0_rec_in = {k: v for k, v in _L0_rec_all.items() if k in ('row', 'col', 'vals', 'emb', 'W1_1', 'b1_1', 'W1_2', 'b1_2', 'W2_1', 'b2_1', 'W2_2', 'b2_2', 'W3_1', 'b3_1', 'W3_2', 'b3_2')}
    del _L0_rec_all
    return {'r_x_ids': r_x_ids, 'L0_rec_row': _L0_rec_in['row'], 'L0_rec_col': _L0_rec_in['col'], 'L0_rec_vals': _L0_rec_in['vals'], 'L0_rec_emb': _L0_rec_in['emb'], 'L0_rec_W1_1': _L0_rec_in['W1_1'], 'L0_rec_b1_1': _L0_rec_in['b1_1'], 'L0_rec_W1_2': _L0_rec_in['W1_2'], 'L0_rec_b1_2': _L0_rec_in['b1_2'], 'L0_rec_W2_1': _L0_rec_in['W2_1'], 'L0_rec_b2_1': _L0_rec_in['b2_1'], 'L0_rec_W2_2': _L0_rec_in['W2_2'], 'L0_rec_b2_2': _L0_rec_in['b2_2'], 'L0_rec_W3_1': _L0_rec_in['W3_1'], 'L0_rec_b3_1': _L0_rec_in['b3_1'], 'L0_rec_W3_2': _L0_rec_in['W3_2'], 'L0_rec_b3_2': _L0_rec_in['b3_2']}

def reference(r_x_ids, L0_rec_row, L0_rec_col, L0_rec_vals, L0_rec_emb, L0_rec_W1_1, L0_rec_b1_1, L0_rec_W1_2, L0_rec_b1_2, L0_rec_W2_1, L0_rec_b2_1, L0_rec_W2_2, L0_rec_b2_2, L0_rec_W3_1, L0_rec_b3_1, L0_rec_W3_2, L0_rec_b3_2):
    import jax
    import jax.numpy as jnp

    def _L0_rec_ref(x_ids, row, col, vals, emb, W1_1, b1_1, W1_2, b1_2, W2_1, b2_1, W2_2, b2_2, W3_1, b3_1, W3_2, b3_2):
        import jax, jax.numpy as jnp
        import numpy as np
        N = 12500
        E = 400000
        D = 128
        NEG_SLOPE = 0.2

        def _spmm(row, col, vals, x):
            msg = vals[:, None] * x[col]
            return jax.ops.segment_sum(msg, row, num_segments=N)

        def _layer(x_prev, row, col, vals, W_a, b_a, W_b, b_b):
            h = _spmm(row, col, vals, x_prev)
            z = (h + x_prev) @ W_a.T + b_a + h * x_prev @ W_b.T + b_b
            return jnp.where(z >= 0, z, NEG_SLOPE * z)
        x = emb[x_ids]
        x1 = _layer(x, row, col, vals, W1_1, b1_1, W1_2, b1_2)
        x2 = _layer(x1, row, col, vals, W2_1, b2_1, W2_2, b2_2)
        x3 = _layer(x2, row, col, vals, W3_1, b3_1, W3_2, b3_2)
        return jnp.concatenate((x, x1, x2, x3), axis=1)
    y = _L0_rec_ref(r_x_ids, L0_rec_row, L0_rec_col, L0_rec_vals, L0_rec_emb, L0_rec_W1_1, L0_rec_b1_1, L0_rec_W1_2, L0_rec_b1_2, L0_rec_W2_1, L0_rec_b2_1, L0_rec_W2_2, L0_rec_b2_2, L0_rec_W3_1, L0_rec_b3_1, L0_rec_W3_2, L0_rec_b3_2)
    return y

_drawn_inputs = setup_inputs


def setup_inputs(seed=0):
    import zlib

    import numpy as np

    out = dict(_drawn_inputs(seed))
    spreads = {'L0_rec_b1_1': (0.0, 0.1),
     'L0_rec_b1_2': (0.0, 0.1),
     'L0_rec_b2_1': (0.0, 0.1),
     'L0_rec_b2_2': (0.0, 0.1),
     'L0_rec_b3_1': (0.0, 2.0),
     'L0_rec_b3_2': (0.0, 2.0)}
    factors = {'L0_rec_W1_2': 64.0}
    for name, (base, spread) in spreads.items():
        noise = np.random.default_rng([zlib.crc32(name.encode()), seed]).standard_normal(out[name].shape)
        drawn = base * np.exp(spread * noise) if base else spread * noise
        out[name] = jnp.asarray(drawn.astype(out[name].dtype))
    for name, factor in factors.items():
        out[name] = (out[name] * factor).astype(out[name].dtype)
    return out
```

```python
from contextlib import ExitStack

import concourse.bass as bass
from concourse import mybir

F32 = mybir.dt.float32
BF16 = mybir.dt.bfloat16
I32 = mybir.dt.int32
ALU = mybir.AluOpType
ACT = mybir.ActivationFunctionType
AX = mybir.AxisListType

P = 128
N = 12500
E = 400000
D = 128
LAYERS = 3
SLOPE = 0.2
DMA = 16

BLK = 250
NB = N // BLK
HALF = BLK // 2
COLS = E // P
GRP = 5
RING = 4
STEP = GRP * RING
TILES = -(-(COLS + NB) // STEP) * STEP
STEPS = TILES // STEP
GROUPS = TILES // GRP

LANES = 25
RANKS = COLS // LANES
BANKL = 10
SR = 5
SOUT = RANKS // SR
OHW = LANES * NB
TAB = -(-TILES // P) * P

XG = 4
XGROUPS = N // (HALF * XG)
XR = RING * GRP // XG
XOUT = XGROUPS // XR

ROUND = 12582912.0


def graph_layers(nc, ids, row, col, vals, emb, weights, biases, out):
    ctx = ExitStack()
    with ctx:
        def sb(name, shape, dt=F32):
            return ctx.enter_context(nc.sbuf_tensor(name, shape, dt))

        def sem(name):
            return ctx.enter_context(nc.semaphore(name))

        sorted_edges = nc.dram_tensor("sorted_edges", [P * TILES, 3], F32, kind="Internal").ap()
        x_now = nc.dram_tensor("x_now", [N, D], F32, kind="Internal").ap()
        tile_offsets = nc.dram_tensor("tile_offsets", [P, TAB // P], I32, kind="Internal").ap()

        hT = sb("hT", [P, N])
        xT = sb("xT", [P, N])
        recs = sb("recs", [P, TILES, 3])
        xg = sb("xg", [P, RING * GRP, D])
        sel = sb("sel", [P, 2 * GRP, BLK])
        oh_tab = sb("oh_tab", [P, TAB])
        ranked = sb("ranked", [P, OHW])
        idx = sb("idx", [P, RING * GRP], I32)
        addr = sb("addr", [P, SR, LANES], I32)
        place = sb("place", [P, 4, LANES])
        stage = sb("stage", [P, SR, LANES, 3])
        w_sb = sb("w_sb", [P, LAYERS, 2, D])
        bias = sb("bias", [1, 3, LAYERS, D])
        iota_w = sb("iota_w", [P, BLK])
        iota_b = sb("iota_b", [P, NB])
        iota_t = sb("iota_t", [P, TAB // P])
        ident = sb("ident", [P, P])
        ones_f = sb("ones_f", [1, P])
        ones_b = sb("ones_b", [P, P], BF16)
        zero_b = sb("zero_b", [P, P], BF16)
        before = sb("before", [P, P], BF16)
        after = sb("after", [P, P], BF16)
        ids_c = sb("ids_c", [N // HALF, HALF], I32)
        ids_f = sb("ids_f", [N // HALF, HALF])
        ids_t = sb("ids_t", [HALF, N // HALF])
        tot_b = sb("tot_b", [P, NB])
        n_tiles = sb("n_tiles", [P, NB])
        end_tile = sb("end_tile", [P, NB])
        tab_f = sb("tab_f", [P, TAB // P])
        tab_i = sb("tab_i", [P, TAB // P], I32)
        ps = ctx.enter_context(nc.psum_tensor("ps", [P, 8, 512], F32))

        flat = recs[:, :, :].rearrange("p t c -> p (t c)")
        raw_row = flat[:, 0:COLS].bitcast(I32)
        raw_col = flat[:, COLS:2 * COLS].bitcast(I32)
        raw_val = flat[:, 2 * COLS:3 * COLS]
        rloc = flat[:, 0:COLS]
        block_of = hT[:, 0:COLS]
        w_raw = hT[:, 4000:4000 + 6 * D].rearrange("p (w d) -> p w d", d=D)
        tot = hT[:, 5000:5000 + OHW].rearrange("p (b l) -> p b l", l=LANES)
        scan_a = hT[:, 6500:6500 + OHW].rearrange("p (b l) -> p b l", l=LANES)
        scan_b = hT[:, 8000:8000 + OHW].rearrange("p (b l) -> p b l", l=LANES)
        base = hT[:, 9500:9500 + OHW].rearrange("p (b l) -> p b l", l=LANES)
        base_l = hT[0:1, 11000:11000 + OHW]
        zeros = sel[:, :, :].rearrange("p s w -> p (s w)")
        ZW = TILES * 3 // 4
        assert ZW <= 2 * GRP * BLK
        oh = oh_tab[:, :].bitcast(BF16)[:, 0:SR * OHW].rearrange("p (r l b) -> p r l b", r=SR, b=NB)
        table = oh_tab[0:1, :].bitcast(I32)
        sumT = [sel[:, 0, :], sel[:, 1, :]]
        prodT = [sel[:, 2, :], sel[:, 3, :]]
        zero_blk = sel[:, 4, :]
        low = [xg[0:HALF, 0:2, :], xg[0:HALF, 2:4, :]]
        x_new = [xg[0:HALF, 4:6, :], xg[0:HALF, 6:8, :]]

        acc = ps[:, 0:3, :]
        part = [ps[:, 3 * g + k // 2, BLK * (k % 2):BLK * (k % 2 + 1)] for g in range(2) for k in range(GRP)]
        zps = [ps[0:HALF, q, 0:2 * D].rearrange("p (h d) -> p h d", h=2) for q in range(2)]
        tps = [ps[:, 2 + q, 0:BLK] for q in range(2)]
        LANE_BANKS = [(0, BANKL), (1, BANKL), (2, LANES - 2 * BANKL)]


        const_ready = sem("const_ready")
        edges_in = sem("edges_in")
        ids_in = sem("ids_in")
        w_in = sem("w_in")
        zero_filled = sem("zero_filled")
        zeros_ready = sem("zeros_ready")
        dve_link = sem("dve_link")
        rank_link = sem("rank_link")
        counted = sem("counted")
        ids_float = sem("ids_float")
        ids_turned = sem("ids_turned")
        ids_ready = sem("ids_ready")
        w_turned = sem("w_turned")
        w_ready = sem("w_ready")
        rloc_ready = sem("rloc_ready")
        onehot_ready = sem("onehot_ready")
        hist_done = sem("hist_done")
        base_ready = sem("base_ready")
        onehot2_ready = sem("onehot2_ready")
        rank_ready = sem("rank_ready")
        rank_read = sem("rank_read")
        addr_ready = sem("addr_ready")
        stage_ready = sem("stage_ready")
        scattered = [sem(f"scattered{r}") for r in range(SR)]
        tab_ready = sem("tab_ready")
        tab_stored = sem("tab_stored")
        tab_in = sem("tab_in")
        recs_in = sem("recs_in")
        x0_idx = sem("x0_idx")
        x0_got = [sem(f"x0_got{q}") for q in range(XR)]
        x0_turned = sem("x0_turned")
        x0_kept = sem("x0_kept")
        x0_stored = [sem(f"x0_stored{q}") for q in range(XR)]
        idx_ready = sem("idx_ready")
        pool_groups = sem("pool_groups")
        gathered = [sem(f"gathered{g}") for g in range(RING)]
        sel_ready = sem("sel_ready")
        part_ready = sem("part_ready")
        part_added = sem("part_added")
        sum_ready = sem("sum_ready")
        prod_ready = sem("prod_ready")
        blk_zeroed = sem("blk_zeroed")
        zconst_ready = sem("zconst_ready")
        z_ready = sem("z_ready")
        low_ready = sem("low_ready")
        new_ready = sem("new_ready")
        new_turned = sem("new_turned")
        xT_ready = sem("xT_ready")
        stored = [sem(f"stored{q}") for q in range(2)]

        CONSTS = 10
        HISTCREDIT = SR
        READYCREDIT = RING
        ADDCREDIT = 2 * GRP

        block = ctx.enter_context(nc.Block())

        @block.gpsimd
        def _(pool):
            g = nc.gpsimd
            g.memset(ident[:, :], 0.0).then_inc(const_ready, 1)
            g.memset(ones_f[:, :], 1.0).then_inc(const_ready, 1)
            g.memset(ones_b[:, :], 1.0).then_inc(const_ready, 1)
            g.memset(zero_b[:, :], 0.0).then_inc(const_ready, 1)
            pool.wait_ge(const_ready, 4)
            g.affine_select(out=ident[:, :], in_=ident[:, :], compare_op=ALU.not_equal, fill=1.0,
                            base=0, pattern=[[-1, P]], channel_multiplier=1).then_inc(const_ready, 1)
            g.affine_select(out=before[:, :], in_=ones_b[:, :], compare_op=ALU.is_gt, fill=0.0,
                            base=0, pattern=[[1, P]], channel_multiplier=-1).then_inc(const_ready, 1)
            g.affine_select(out=after[:, :], in_=ones_b[:, :], compare_op=ALU.is_ge, fill=0.0,
                            base=0, pattern=[[-1, P]], channel_multiplier=1).then_inc(const_ready, 1)
            g.iota(iota_b[:, :], pattern=[[1, NB]], base=0, channel_multiplier=0,
                   allow_small_or_imprecise_dtypes=True).then_inc(const_ready, 1)
            g.iota(iota_w[:, :], pattern=[[1, BLK]], base=0, channel_multiplier=0,
                   allow_small_or_imprecise_dtypes=True).then_inc(const_ready, 1)
            g.iota(iota_t[:, :], pattern=[[1, TAB // P]], base=0, channel_multiplier=TAB // P,
                   allow_small_or_imprecise_dtypes=True).then_inc(const_ready, 1)

            pool.sem_inc(hist_done, HISTCREDIT)
            pool.sem_inc(x0_kept, 1)
            pool.sem_inc(part_ready, READYCREDIT)
            pool.sem_inc(part_added, ADDCREDIT)

            def taken_up():
                pool.sem_inc(pool_groups, 1)

            with pool.Fori(0, XOUT) as j:
                for q in range(XR):
                    pool.wait_ge(x0_idx, j * XR + (q + 1))
                    taken_up()
                    for k in range(q * XG, q * XG + XG):
                        pool.indirect_dma_start(
                            out=xg[0:HALF, k, :], out_offset=None, in_=emb,
                            in_offset=bass.IndirectOffsetOnAxis(ap=idx[0:HALF, k:k + 1], axis=0),
                        ).then_inc(x0_got[q], DMA)

            pool.wait_ge(zero_filled, 4 * DMA)
            with pool.Fori(0, SOUT) as j:
                for r in range(SR):
                    pool.wait_ge(addr_ready, j * SR + (r + 1))
                    pool.wait_ge(stage_ready, j * SR + (r + 1))
                    taken_up()
                    for k in range(LANES):
                        pool.indirect_dma_start(
                            out=sorted_edges,
                            out_offset=bass.IndirectOffsetOnAxis(ap=addr[:, r, k:k + 1], axis=0),
                            in_=stage[:, r, k, :], in_offset=None,
                        ).then_inc(scattered[r], DMA)

            for q in range(XR):
                pool.wait_ge(x0_stored[q], XOUT * 2 * DMA)
            with pool.Fori(0, LAYERS) as la:
                with pool.Fori(0, STEPS) as i:
                    for gr in range(RING):
                        pool.wait_ge(idx_ready, la * GROUPS + i * RING + (gr + 1))
                        taken_up()
                        for k in range(gr * GRP, gr * GRP + GRP):
                            pool.indirect_dma_start(
                                out=xg[:, k, :], out_offset=None, in_=x_now,
                                in_offset=bass.IndirectOffsetOnAxis(ap=idx[:, k:k + 1], axis=0),
                            ).then_inc(gathered[gr], DMA)
                pool.wait_ge(part_added, ADDCREDIT + la * TILES + TILES)
                pool.wait_ge(part_ready, READYCREDIT + la * GROUPS + GROUPS)

                def dense_pair(j, first):
                    for q in range(2):
                        if not first:
                            pool.wait_ge(z_ready, la * NB + j * 2 + (q - 1))
                        blk = bass.ds(j * (2 * BLK) + q * BLK, BLK)
                        g.tensor_tensor(prodT[q], hT[:, blk], xT[:, blk], ALU.mult).then_inc(prod_ready, 1)

                dense_pair(0, True)
                with pool.Fori(1, NB // 2) as j:
                    dense_pair(j, False)
                for q in range(2):
                    pool.wait_ge(stored[q], la * (NB * DMA) + NB * DMA)

        @block.sync
        def _(sp):
            for k, src in enumerate((row, col, vals)):
                dst = (raw_row, raw_col, raw_val)[k]
                sp.dma_start(dst, src.rearrange("(p c) -> p c", p=P)).then_inc(edges_in, DMA)
            sp.dma_start(ids_c[:, :], ids.rearrange("(c r) -> c r", r=HALF)).then_inc(ids_in, DMA)
            for k, w in enumerate(weights):
                sp.dma_start(w_raw[:, k, :], w).then_inc(w_in, DMA)
            for k, b in enumerate(biases):
                sp.dma_start(bias[0:1, 1 + k % 2, k // 2, :], b.rearrange("(a d) -> a d", a=1)).then_inc(w_in, DMA)
            sp.wait_ge(zeros_ready, 1)
            fill = sorted_edges.rearrange("(p t) c -> p (t c)", p=P)
            for k in range(4):
                sp.dma_start(fill[:, k * ZW:(k + 1) * ZW], zeros[:, 0:ZW]).then_inc(zero_filled, DMA)

            x0_out = out.rearrange("(n k r) f -> n r k f", k=XG, r=HALF)
            x0_now = x_now.rearrange("(n k r) f -> n r k f", k=XG, r=HALF)
            with sp.Fori(0, XOUT) as j:
                for q in range(XR):
                    sp.wait_ge(x0_got[q], j * (XG * DMA) + XG * DMA)
                    sp.dma_start(x0_out[bass.ds(j * XR + q, 1), :, :, 0:D].rearrange("a r k f -> (a r) k f"),
                                 xg[0:HALF, q * XG:q * XG + XG, :]).then_inc(x0_stored[q], DMA)
                    sp.dma_start(x0_now[bass.ds(j * XR + q, 1), :, :, :].rearrange("a r k f -> (a r) k f"),
                                 xg[0:HALF, q * XG:q * XG + XG, :]).then_inc(x0_stored[q], DMA)

            sp.wait_ge(tab_ready, 1)
            sp.dma_start(tile_offsets, tab_i[:, :]).then_inc(tab_stored, DMA)
            sp.wait_ge(tab_stored, DMA)
            for r in range(SR):
                sp.wait_ge(scattered[r], SOUT * LANES * DMA)
            sp.dma_start(recs[:, :, :], sorted_edges.rearrange("(p t) c -> p t c", p=P)).then_inc(recs_in, DMA)
            sp.wait_ge(counted, RANKS)
            sp.dma_start(table, tile_offsets.rearrange("p t -> (p t)").rearrange("(a t) -> a t", a=1)).then_inc(tab_in, DMA)

            new_out = out.rearrange("(n h r) (l d) -> n l r h d", h=2, r=HALF, d=D)
            new_now = x_now.rearrange("(n h r) d -> n r h d", h=2, r=HALF)
            with sp.Fori(0, LAYERS) as la:
                with sp.Fori(0, NB // 2) as j:
                    for q in range(2):
                        sp.wait_ge(new_ready, la * NB + j * 2 + (q + 1))
                        sp.dma_start(
                            new_out[bass.ds(j * 2 + q, 1), bass.ds(la + 1, 1), :, :, :].rearrange("a b r h d -> (a b r) h d"),
                            x_new[q]).then_inc(stored[q], DMA)
                        sp.dma_start(new_now[bass.ds(j * 2 + q, 1), :, :, :].rearrange("a r h d -> (a r) h d"),
                                     x_new[q]).then_inc(stored[q], DMA)
            for q in range(2):
                sp.wait_ge(stored[q], LAYERS * (NB // 2) * 2 * DMA)

        @block.scalar
        def _(act):
            s = nc.scalar
            act.wait_ge(const_ready, CONSTS)
            act.wait_ge(ids_ready, 1)

            def x0_index(col0, q):
                s.activation(idx[0:HALF, q * XG:q * XG + XG], ids_t[:, col0], ACT.Copy).then_inc(x0_idx, 1)

            def x0_keep(n, count):
                act.wait_ge(x0_turned, count)
                s.activation(xT[:, bass.ds(n * (XG * HALF), XG * HALF)], ps[:, 3, 0:XG * HALF], ACT.Copy).then_inc(x0_kept, 1)

            for n in range(XR - 1):
                x0_index(slice(n * XG, n * XG + XG), n)
            x0_keep(0, 1)
            x0_index(slice((XR - 1) * XG, XR * XG), XR - 1)
            with act.Fori(0, XOUT - 1) as j:
                for q in range(XR):
                    x0_keep(j * XR + (q + 1), j * XR + (q + 2))
                    act.wait_ge(x0_stored[q], j * (2 * DMA) + 2 * DMA)
                    x0_index(bass.ds(j * (XR * XG) + (XR + q) * XG, XG), q)
            for n in range(XGROUPS - XR + 1, XGROUPS):
                x0_keep(n, n + 1)

            act.wait_ge(edges_in, 3 * DMA)
            act.wait_ge(rloc_ready, 1)

            def stage_records(it, r):
                c = bass.ds(it * LANES, LANES)
                s.activation(stage[:, r, :, 0], raw_col[:, c], ACT.Copy)
                s.activation(stage[:, r, :, 1], rloc[:, c], ACT.Copy)
                s.activation(stage[:, r, :, 2], raw_val[:, c], ACT.Copy).then_inc(stage_ready, 1)

            for r in range(SR):
                stage_records(r, r)
            with act.Fori(1, SOUT) as j:
                for r in range(SR):
                    act.wait_ge(scattered[r], j * (LANES * DMA))
                    stage_records(j * SR + r, r)

            act.wait_ge(recs_in, DMA)
            with act.Fori(0, LAYERS) as la:
                with act.Fori(0, STEPS) as i:
                    for gr in range(RING):
                        act.wait_ge(part_ready, la * GROUPS + i * RING + (gr + 1))
                        s.activation(idx[:, gr * GRP:gr * GRP + GRP], recs[:, bass.ds(i * STEP + gr * GRP, GRP), 0],
                                     ACT.Copy).then_inc(idx_ready, 1)

                def dense_pair(j, first):
                    n = la * NB + j * 2
                    for q in range(2):
                        act.wait_ge(z_ready, n + (q + 1))
                        if not first:
                            act.wait_ge(new_ready, n + (q - 1))
                        s.activation(low[q], zps[q], ACT.Copy, scale=SLOPE).then_inc(low_ready, 1)
                    if first:
                        act.wait_ge(zconst_ready, la + 1)
                    for q in range(2):
                        blk = bass.ds(j * (2 * BLK) + q * BLK, BLK)
                        s.activation(hT[:, blk], zero_blk, ACT.Copy).then_inc(blk_zeroed, 1)
                    for q in range(2):
                        blk = bass.ds(j * (2 * BLK) + q * BLK, BLK)
                        act.wait_ge(new_turned, n + (q + 1))
                        s.activation(xT[:, blk], tps[q], ACT.Copy).then_inc(xT_ready, 1)

                dense_pair(0, True)
                with act.Fori(1, NB // 2) as j:
                    dense_pair(j, False)

        @block.tensor
        def _(pe):
            t = nc.tensor
            pe.wait_ge(const_ready, CONSTS)
            pe.wait_ge(w_in, 4 * LAYERS * DMA)
            for k in range(2 * LAYERS):
                last = t.transpose(ps[:, 5 + k // 4, (k % 4) * D:(k % 4 + 1) * D], w_raw[:, k, :], ident[:, :])
            last.then_inc(w_turned, 1)
            pe.wait_ge(ids_float, 1)
            t.transpose(ps[0:HALF, 7, 0:N // HALF], ids_f[:, :], ident[0:N // HALF, 0:N // HALF]).then_inc(ids_turned, 1)

            pe.wait_ge(zeros_ready, 1)
            zb = zeros.bitcast(BF16)
            for a, lanes in LANE_BANKS:
                t.matmul(acc[:, a, 0:lanes * NB], zero_b[:, :], zb[:, 0:lanes * NB], start=True, stop=True)

            def hist(it, r):
                pe.wait_ge(onehot_ready, it + 1)
                for a, lanes in LANE_BANKS:
                    last = t.matmul(acc[:, a, 0:lanes * NB], ones_b[:, :],
                                    oh[:, r, a * BANKL:a * BANKL + lanes, :].rearrange("p l b -> p (l b)"),
                                    start=False, stop=True, skip_group_check=True)
                last.then_inc(hist_done, 1)

            with pe.Fori(0, XOUT) as j:
                for q in range(XR):
                    for r in range(SR):
                        hist(j * (XR * SR) + (q * SR + r), r)
                    pe.wait_ge(x0_got[q], j * (XG * DMA) + XG * DMA)
                    pe.wait_ge(x0_kept, j * XR + (q + 1))
                    for k in range(XG):
                        last = t.transpose(ps[:, 3, k * HALF:(k + 1) * HALF], xg[0:HALF, q * XG + k, :], ident[0:HALF, 0:HALF])
                    last.then_inc(x0_turned, 1)

            pe.wait_ge(base_ready, 1)
            for a, lanes in LANE_BANKS:
                t.matmul(acc[:, a, 0:lanes * NB], ones_f[0:1, :],
                         base_l[:, a * BANKL * NB:(a * BANKL + lanes) * NB], start=True, stop=True)
            with pe.Fori(0, SOUT) as j:
                for r in range(SR):
                    pe.wait_ge(onehot2_ready, j * SR + (r + 1))
                    for stage_, lhs in enumerate((before, after)):
                        if stage_:
                            pe.wait_ge(rank_read, j * SR + (r + 1))
                        for a, lanes in LANE_BANKS:
                            last = t.matmul(acc[:, a, 0:lanes * NB], lhs[:, :],
                                            oh[:, r, a * BANKL:a * BANKL + lanes, :].rearrange("p l b -> p (l b)"),
                                            start=False, stop=True, skip_group_check=True)
                        last.then_inc(counted if stage_ else rank_ready, 1)

            pe.wait_ge(w_ready, 1)
            with pe.Fori(0, LAYERS) as la:
                with pe.Fori(0, STEPS) as i:
                    for gr in range(RING):
                        n = la * GROUPS + i * RING
                        pe.wait_ge(gathered[gr], la * (STEPS * GRP * DMA) + i * (GRP * DMA) + GRP * DMA)
                        pe.wait_ge(sel_ready, n + (gr + 1))
                        pe.wait_ge(part_added, la * TILES + i * STEP + (gr + 1) * GRP)
                        for k in range(GRP):
                            last = t.matmul(part[(gr % 2) * GRP + k], xg[:, gr * GRP + k, :],
                                            sel[:, (gr % 2) * GRP + k, :], start=True, stop=True)
                        last.then_inc(part_ready, 1)

                def dense_pair(j, first):
                    n = la * NB + j * 2
                    for q in range(2):
                        pe.wait_ge(sum_ready, n + (q + 1))
                        pe.wait_ge(prod_ready, n + (q + 1))
                        if not first:
                            pe.wait_ge(new_ready, n + (q - 1))
                        for h in range(2):
                            rows = slice(h * HALF, (h + 1) * HALF)
                            t.matmul(zps[q][:, h, :], sumT[q][:, rows], w_sb[:, bass.ds(la, 1), 0, :].rearrange("p a d -> p (a d)"), start=True, stop=False)
                            t.matmul(zps[q][:, h, :], prodT[q][:, rows], w_sb[:, bass.ds(la, 1), 1, :].rearrange("p a d -> p (a d)"), start=False, stop=False)
                            last = t.matmul(zps[q][:, h, :], ones_f[0:1, 0:HALF], bias[0:1, 0, bass.ds(la, 1), :].rearrange("p a d -> p (a d)"),
                                            start=False, stop=True)
                        last.then_inc(z_ready, 1)
                    for q in range(2):
                        pe.wait_ge(new_ready, n + (q + 1))
                        if not first:
                            pe.wait_ge(xT_ready, n + (q - 1))
                        for h in range(2):
                            last = t.transpose(tps[q][:, h * HALF:(h + 1) * HALF], x_new[q][:, h, :], ident[0:HALF, 0:HALF])
                        last.then_inc(new_turned, 1)

                dense_pair(0, True)
                with pe.Fori(1, NB // 2) as j:
                    dense_pair(j, False)

        @block.vector
        def _(dve):
            v = nc.vector
            links = [0]

            def link(ins):
                links[0] += 1
                ins.then_inc(dve_link, 1)
                dve.wait_ge(dve_link, links[0])

            v.memset(zeros, 0.0).then_inc(zeros_ready, 1)
            dve.wait_ge(ids_in, DMA)
            v.tensor_copy(ids_f[:, :], ids_c[:, :]).then_inc(ids_float, 1)
            dve.wait_ge(ids_turned, 1)
            v.tensor_copy(ids_t[:, :], ps[0:HALF, 7, 0:N // HALF]).then_inc(ids_ready, 1)

            dve.wait_ge(edges_in, 3 * DMA)
            link(v.tensor_scalar(block_of, raw_row, -(BLK - 1) / 2, 1.0 / BLK, ALU.add, ALU.mult))
            link(v.tensor_scalar(block_of, block_of, ROUND, -ROUND, ALU.add, ALU.add))
            v.scalar_tensor_tensor(rloc, block_of, -float(BLK), raw_row, ALU.mult, ALU.add).then_inc(rloc_ready, 1)

            dve.wait_ge(const_ready, CONSTS)

            def one_hot(it, r):
                return v.tensor_tensor(oh[:, r, :, :],
                                       block_of[:, bass.ds(it * LANES, LANES)][:, :, None].to_broadcast([P, LANES, NB]),
                                       iota_b[:, None, :].to_broadcast([P, LANES, NB]), ALU.is_equal)

            with dve.Fori(0, SOUT) as j:
                for r in range(SR):
                    dve.wait_ge(hist_done, j * SR + (r + 1))
                    one_hot(j * SR + r, r).then_inc(onehot_ready, 1)

            dve.wait_ge(w_turned, 1)
            wf = w_sb[:, :, :, :].rearrange("p l k d -> p (l k d)")
            v.tensor_copy(wf[:, 0:4 * D], ps[:, 5, 0:4 * D])
            v.tensor_copy(wf[:, 4 * D:6 * D], ps[:, 6, 0:2 * D])
            v.tensor_tensor(bias[0:1, 0, :, :], bias[0:1, 1, :, :], bias[0:1, 2, :, :], ALU.add).then_inc(w_ready, 1)

            dve.wait_ge(hist_done, RANKS + SR)
            v.tensor_copy(tot[:, :, 0:2 * BANKL].rearrange("p b (a l) -> p a l b", a=2),
                          acc[:, 0:2, 0:BANKL * NB].rearrange("p a (l b) -> p a l b", b=NB))
            link(v.tensor_copy(tot[:, :, 2 * BANKL:LANES].rearrange("p b l -> p l b"),
                               acc[:, 2, 0:(LANES - 2 * BANKL) * NB].rearrange("p (l b) -> p l b", b=NB)))
            link(v.tensor_reduce(tot_b[:, :], tot, AX.X, ALU.add))
            link(v.tensor_scalar(n_tiles[:, :], tot_b[:, :], (P - 1) / 2, 1.0 / P, ALU.add, ALU.mult))
            link(v.tensor_scalar(n_tiles[:, :], n_tiles[:, :], ROUND, -ROUND, ALU.add, ALU.add))
            link(v.memset(tot_b[:, :], 1.0))
            link(v.tensor_tensor_scan(end_tile[:, :], tot_b[:, :], n_tiles[:, :], 0.0, ALU.mult, ALU.add))
            link(v.memset(scan_a, 1.0))
            v.memset(scan_a[:, :, 0:1], 0.0)
            v.tensor_copy(scan_b[:, :, 1:LANES], tot[:, :, 0:LANES - 1])
            link(v.tensor_tensor(tot_b[:, :], end_tile[:, :], n_tiles[:, :], ALU.subtract))
            link(v.tensor_scalar(scan_b[:, :, 0], tot_b[:, :], float(P), None, ALU.mult))
            link(v.tensor_tensor_scan(base.rearrange("p b l -> p (b l)"), scan_a.rearrange("p b l -> p (b l)"),
                                      scan_b.rearrange("p b l -> p (b l)"), 0.0, ALU.mult, ALU.add))
            v.tensor_copy(base_l.rearrange("p (l b) -> p b l", b=NB), base[0:1, :, :]).then_inc(base_ready, 1)
            big = ranked[:, :].rearrange("p (t b) -> p t b", b=NB)
            link(v.tensor_tensor(big, iota_t[:, :, None].to_broadcast([P, TAB // P, NB]),
                                 end_tile[:, None, :].to_broadcast([P, TAB // P, NB]), ALU.is_ge))
            link(v.tensor_reduce(tab_f[:, :], big, AX.X, ALU.add))
            v.tensor_scalar(tab_i[:, :], tab_f[:, :], float(NB - 1), float(BLK), ALU.min, ALU.mult).then_inc(tab_ready, 1)

            step_links = [0]

            def rank_step(it, r, j, first):
                def chain(ins):
                    step_links[0] += 1
                    ins.then_inc(rank_link, 1)
                    dve.wait_ge(rank_link, it * 4 + step_links[0])

                step_links[0] = 0
                dve.wait_ge(rank_ready, it + 1)
                v.tensor_tensor(ranked[:, 0:2 * BANKL * NB].rearrange("p (a x) -> p a x", a=2), acc[:, 0:2, 0:BANKL * NB],
                                oh[:, r, 0:2 * BANKL, :].rearrange("p (a l) b -> p a (l b)", a=2), ALU.mult)
                v.tensor_tensor(ranked[:, 2 * BANKL * NB:OHW], acc[:, 2, 0:(LANES - 2 * BANKL) * NB],
                                oh[:, r, 2 * BANKL:LANES, :].rearrange("p l b -> p (l b)"), ALU.mult).then_inc(rank_read, 1)
                dve.wait_ge(rank_read, it + 1)
                chain(v.tensor_reduce(place[:, 0, :], ranked[:, :].rearrange("p (l b) -> p l b", b=NB), AX.X, ALU.add))
                chain(v.tensor_scalar(place[:, 1, :], place[:, 0, :], -(P - 1) / 2, 1.0 / P, ALU.add, ALU.mult))
                chain(v.tensor_scalar(place[:, 2, :], place[:, 1, :], ROUND, -ROUND, ALU.add, ALU.add))
                chain(v.scalar_tensor_tensor(place[:, 3, :], place[:, 2, :], -float(P), place[:, 0, :], ALU.mult, ALU.add))
                if not first:
                    dve.wait_ge(scattered[r], j * (LANES * DMA))
                v.scalar_tensor_tensor(addr[:, r, :], place[:, 3, :], float(TILES), place[:, 2, :],
                                       ALU.mult, ALU.add).then_inc(addr_ready, 1)

            def rank_round(j, first):
                for r in range(SR):
                    one_hot(j * SR + r, r).then_inc(onehot2_ready, 1)
                    rank_step(j * SR + r, r, j, first)

            rank_round(0, True)
            with dve.Fori(1, SOUT) as j:
                rank_round(j, False)

            link(v.memset(hT[:, :], 0.0))
            dve.wait_ge(recs_in, DMA)
            dve.wait_ge(tab_in, DMA)
            with dve.Fori(0, LAYERS) as la:
                def select(t0, gr, k):
                    slot = (gr % 2) * GRP + k
                    at = bass.ds(t0 + (gr * GRP + k), 1)
                    return v.tensor_scalar(sel[:, slot, :], iota_w[:, :], recs[:, at, 1], recs[:, at, 2],
                                           ALU.is_equal, ALU.mult)

                def step(t0, i, last_step):
                    for gr in range(RING):
                        _, offs = nc.values_load_multi_w_load_instructions(
                            table[0:1, bass.ds(t0 + gr * GRP, GRP)], engines=[mybir.EngineType.DVE],
                            min_val=0, max_val=N - BLK, skip_runtime_bounds_check_because="the table holds offsets of blocks")
                        dve.wait_ge(part_ready, la * GROUPS + i * RING + (READYCREDIT + gr + 1))
                        for k in range(GRP):
                            dve.wait_ge(part_added, la * TILES + i * STEP + (ADDCREDIT + gr * GRP + k))
                            blk = hT[:, bass.ds(offs[k], BLK)]
                            v.tensor_tensor(blk, blk, part[(gr % 2) * GRP + k], ALU.add).then_inc(part_added, 1)
                            if not (last_step and gr >= RING - 2):
                                built = select(t0, gr + 2, k)
                                if k == GRP - 1:
                                    built.then_inc(sel_ready, 1)

                for gr in range(2):
                    for k in range(GRP):
                        built = select(0, gr, k)
                    built.then_inc(sel_ready, 1)
                with dve.Fori(0, STEPS - 1) as i:
                    step(i * STEP, i, False)
                step((STEPS - 1) * STEP, STEPS - 1, True)

                dve.wait_ge(part_added, la * TILES + (ADDCREDIT + TILES))
                v.memset(zero_blk, 0.0).then_inc(zconst_ready, 1)

                def dense_pair(j, first):
                    n = la * NB + j * 2
                    for q in range(2):
                        blk = bass.ds(j * (2 * BLK) + q * BLK, BLK)
                        if not first:
                            dve.wait_ge(z_ready, n + (q - 1))
                        v.tensor_tensor(sumT[q], hT[:, blk], xT[:, blk], ALU.add).then_inc(sum_ready, 1)
                    for q in range(2):
                        dve.wait_ge(low_ready, n + (q + 1))
                        if not first:
                            dve.wait_ge(new_turned, n + (q - 1))
                            dve.wait_ge(stored[q], la * (NB * DMA) + j * (2 * DMA))
                        v.tensor_tensor(x_new[q], zps[q], low[q], ALU.max).then_inc(new_ready, 1)

                dense_pair(0, True)
                with dve.Fori(1, NB // 2) as j:
                    dense_pair(j, False)
                dve.wait_ge(blk_zeroed, la * NB + NB)


_INS = ["r_x_ids", "L0_rec_row", "L0_rec_col", "L0_rec_vals", "L0_rec_emb"]
_LAYERS = [("L0_rec_W%d_%d" % (la, k), "L0_rec_b%d_%d" % (la, k)) for la in (1, 2, 3) for k in (1, 2)]


def kernel(**inputs):
    import numpy as np
    import concourse.bacc as bacc
    from concourse.bass_utils import run_bass_kernel_spmd

    nc = bacc.Bacc("TRN2", target_bir_lowering=False, num_devices=1)
    arrays, aps = {}, {}
    for name in _INS + [n for pair in _LAYERS for n in pair]:
        a = np.ascontiguousarray(inputs[name])
        arrays["in_" + name] = a
        aps[name] = nc.dram_tensor("in_" + name, a.shape, mybir.dt.from_np(a.dtype), kind="ExternalInput").ap()
    out = nc.dram_tensor("out_x", (N, D * (LAYERS + 1)), F32, kind="ExternalOutput").ap()
    graph_layers(nc, *[aps[n] for n in _INS], [aps[w] for w, _ in _LAYERS], [aps[b] for _, b in _LAYERS], out)
    r = run_bass_kernel_spmd(nc, [arrays], core_ids=[0])
    return r.results[0]["out_x"]
```

```python
from contextlib import ExitStack

import concourse.bass as bass
from concourse import mybir

F32 = mybir.dt.float32
BF16 = mybir.dt.bfloat16
I32 = mybir.dt.int32
ALU = mybir.AluOpType
ACT = mybir.ActivationFunctionType
AX = mybir.AxisListType

P = 128
N = 12500
E = 400000
D = 128
LAYERS = 3
SLOPE = 0.2
DMA = 16

BLK = 250
NB = N // BLK
HALF = BLK // 2
COLS = E // P
GRP = 5
RING = 4
STEP = GRP * RING
TILES = -(-(COLS + NB) // STEP) * STEP
STEPS = TILES // STEP
GROUPS = TILES // GRP

LANES = 25
CHUNKS = COLS // LANES
BANKL = 10
SR = 5
SOUT = CHUNKS // SR
PAIRS = CHUNKS // 2
OHW = LANES * NB
TABW = -(-TILES // P)
TAB = TABW * P
RUN = 8
RUNS = 4
SLOTS = RUN * RUNS
assert LANES * P + NB * 2 * (RUN - 1) <= P * SLOTS
DUMP = TAB * P // RUN
PACK = 256.0
QHI = 16.0
OPW = LANES * P

XG = 4
XGROUPS = N // (HALF * XG)
XR = RING * GRP // XG
XOUT = XGROUPS // XR

ROUND = 12582912.0


def graph_layers(nc, ids, row, col, vals, emb, weights, biases, out):
    ctx = ExitStack()
    with ctx:
        def sb(name, shape, dt=F32):
            return ctx.enter_context(nc.sbuf_tensor(name, shape, dt))

        def sem(name):
            return ctx.enter_context(nc.semaphore(name))

        sorted_edges = nc.dram_tensor("sorted_edges", [DUMP + RUNS * P, RUN * 2], F32, kind="Internal").ap()
        chunk_places = nc.dram_tensor("chunk_places", [2, CHUNKS * NB], BF16, kind="Internal").ap()
        x_now = nc.dram_tensor("x_now", [N, D], F32, kind="Internal").ap()
        tile_offsets = nc.dram_tensor("tile_offsets", [P, TAB // P], I32, kind="Internal").ap()

        hT = sb("hT", [P, N])
        xT = sb("xT", [P, N])
        recs = sb("recs", [P, 3, TAB])
        xg = sb("xg", [P, RING * GRP, D])
        sel = sb("sel", [P, 2 * GRP, BLK])
        oh_tab = sb("oh_tab", [P, TAB])
        ranked = sb("ranked", [P, OHW])
        idx = sb("idx", [P, RING * GRP], I32)
        run_idx = sb("run_idx", [P, 2, RUNS], I32)
        run_tab = sb("run_tab", [P, RUNS, CHUNKS])
        place = sb("place", [P, 4, LANES])
        stage = sb("stage", [P, 2, SLOTS, 2])
        first10 = sb("first10", [P, 2, NB], BF16)
        w_sb = sb("w_sb", [P, LAYERS, 2, D])
        bias = sb("bias", [1, 3, LAYERS, D])
        iota_w = sb("iota_w", [P, BLK])
        iota_b = sb("iota_b", [P, NB])
        iota_p = sb("iota_p", [P, P])
        iota_run = sb("iota_run", [P, RUNS * P])
        iota_t = sb("iota_t", [P, TAB // P])
        ident = sb("ident", [P, P])
        ones_f = sb("ones_f", [P, P])
        before_f = sb("before_f", [P, P])
        ones_b = sb("ones_b", [P, P], BF16)
        to_row = sb("to_row", [P, 2 * CHUNKS - 1], BF16)
        before = sb("before", [P, P], BF16)
        ids_c = sb("ids_c", [N // HALF, HALF], I32)
        ids_f = sb("ids_f", [N // HALF, HALF])
        ids_t = sb("ids_t", [HALF, N // HALF])
        small = sb("small", [P, 14, NB + 1])
        tab_f = sb("tab_f", [P, TAB // P])
        tab_i = sb("tab_i", [P, TAB // P], I32)
        places_hl = sb("places_hl", [CHUNKS, 2, NB], BF16)
        ps = ctx.enter_context(nc.psum_tensor("ps", [P, 8, 512], F32))

        flat = recs[:, :, :].rearrange("p c t -> p (c t)")
        raw_row = flat[:, 0:COLS].bitcast(I32)
        raw_col = flat[:, COLS:2 * COLS].bitcast(I32)
        raw_val = flat[:, 2 * COLS:3 * COLS]
        packed = flat[:, 0:COLS]
        hb = hT[:, :].bitcast(BF16)
        block_of = hb[:, 0:COLS]
        OP0 = (COLS + 1) // 2
        to_part = [hT[:, OP0 + q * OPW:OP0 + (q + 1) * OPW].rearrange("p (l m) -> p l m", m=P) for q in range(2)]
        QB0 = OP0 + 2 * OPW
        places = hb[0:2, 2 * QB0:2 * QB0 + CHUNKS * NB]
        W0 = QB0 + (CHUNKS * NB + 1) // 2
        assert W0 + 6 * D <= N
        w_raw = hT[:, W0:W0 + 6 * D].rearrange("p (w d) -> p w d", d=D)
        counts = to_part[0].rearrange("p l m -> p (l m)")[0:CHUNKS, 0:OHW].rearrange("p (b l) -> p b l", l=LANES)
        run_to = hT[0:CHUNKS, OP0 + OPW:OP0 + OPW + RUNS * P]
        run_add = hT[0:CHUNKS, OP0 + OPW + RUNS * P:OP0 + OPW + 2 * RUNS * P]
        unsorted = hT[:, 0:TABW * P * 2].rearrange("p (g l f) -> p g l f", l=P, f=2)
        zeros = sel[:, :, :].rearrange("p s w -> p (s w)")
        ZW = (DUMP + RUNS * P) * RUN * 2 // P // 4
        assert ZW <= 2 * GRP * BLK
        ohb = oh_tab[:, :].bitcast(BF16)
        oh = ohb[:, 0:SR * OHW].rearrange("p (r l b) -> p r l b", r=SR, b=NB)
        SLOTW = LANES * SLOTS
        in_slot = oh_tab[:, OHW:OHW + SLOTW].rearrange("p (l c) -> p l c", c=SLOTS)
        moved = [m[:, 0:2 * SLOTW].rearrange("p (l f c) -> p l f c", f=2, c=SLOTS)
                 for m in (zeros, xg[:, :, :].rearrange("p s d -> p (s d)"))]
        table = oh_tab[0:1, :].bitcast(I32)
        sumT = [sel[:, 0, :], sel[:, 1, :]]
        prodT = [sel[:, 2, :], sel[:, 3, :]]
        zero_blk = sel[:, 4, :]
        low = [xg[0:HALF, 0:2, :], xg[0:HALF, 2:4, :]]
        x_new = [xg[0:HALF, 4:6, :], xg[0:HALF, 6:8, :]]

        acc = ps[0:CHUNKS, 0:3, :]
        part = [ps[:, 3 * g + k // 2, BLK * (k % 2):BLK * (k % 2 + 1)] for g in range(2) for k in range(GRP)]
        zps = [ps[0:HALF, q, 0:2 * D].rearrange("p (h d) -> p h d", h=2) for q in range(2)]
        tps = [ps[:, 2 + q, 0:BLK] for q in range(2)]
        LANE_BANKS = [(0, BANKL), (1, BANKL), (2, LANES - 2 * BANKL)]


        const_ready = sem("const_ready")
        edges_in = sem("edges_in")
        ids_in = sem("ids_in")
        w_in = sem("w_in")
        zero_filled = sem("zero_filled")
        zeros_ready = sem("zeros_ready")
        dve_link = sem("dve_link")
        rank_link = sem("rank_link")
        sum_link = sem("sum_link")
        slot_link = sem("slot_link")
        ids_float = sem("ids_float")
        ids_turned = sem("ids_turned")
        ids_ready = sem("ids_ready")
        w_turned = sem("w_turned")
        w_ready = sem("w_ready")
        packed_ready = sem("packed_ready")
        onehot_ready = sem("onehot_ready")
        hist_done = sem("hist_done")
        counts_ready = sem("counts_ready")
        sums_ready = sem("sums_ready")
        places_ready = sem("places_ready")
        places_stored = sem("places_stored")
        places_in = sem("places_in")
        run_link = sem("run_link")
        run_to_ready = sem("run_to_ready")
        run_turned = sem("run_turned")
        run_tab_ready = sem("run_tab_ready")
        onehot2_ready = sem("onehot2_ready")
        rank_ready = sem("rank_ready")
        rank_read = sem("rank_read")
        moved_ready = sem("moved_ready")
        ordered = sem("ordered")
        stage_ready = sem("stage_ready")
        scattered = [sem(f"scattered{q}") for q in range(2)]
        turned = sem("turned")
        turned_kept = [sem(f"turned_kept{f}") for f in range(2)]
        col_ready = sem("col_ready")
        tab_ready = sem("tab_ready")
        tab_stored = sem("tab_stored")
        tab_in = sem("tab_in")
        recs_in = sem("recs_in")
        x0_idx = sem("x0_idx")
        x0_got = [sem(f"x0_got{q}") for q in range(XR)]
        x0_turned = sem("x0_turned")
        x0_kept = sem("x0_kept")
        x0_stored = [sem(f"x0_stored{q}") for q in range(XR)]
        idx_ready = sem("idx_ready")
        pool_groups = sem("pool_groups")
        gathered = [sem(f"gathered{g}") for g in range(RING)]
        sel_ready = sem("sel_ready")
        part_ready = sem("part_ready")
        part_added = sem("part_added")
        sum_ready = sem("sum_ready")
        prod_ready = sem("prod_ready")
        blk_zeroed = sem("blk_zeroed")
        zconst_ready = sem("zconst_ready")
        z_ready = sem("z_ready")
        low_ready = sem("low_ready")
        new_ready = sem("new_ready")
        new_turned = sem("new_turned")
        xT_ready = sem("xT_ready")
        stored = [sem(f"stored{q}") for q in range(2)]

        CONSTS = 13
        HISTCREDIT = SR
        READYCREDIT = RING
        ADDCREDIT = 2 * GRP

        TURNS = [(f, g0, min(g0 + 4, TABW)) for g0 in range(0, TABW, 4) for f in range(2)]

        def keep_turned(eng, copy, field, *how):
            rows = recs[:, 2 * field, :].rearrange("p (t g) -> p g t", g=TABW)
            for m, (f, g0, g1) in enumerate(TURNS):
                if f == field:
                    eng.wait_ge(turned, m + 1)
                    copy(rows[:, g0:g1, :], ps[:, m % 8, 0:(g1 - g0) * P].rearrange("p (g t) -> p g t", t=P),
                         *how).then_inc(turned_kept[f], 1)

        block = ctx.enter_context(nc.Block())

        @block.gpsimd
        def _(pool):
            g = nc.gpsimd
            g.memset(ident[:, :], 0.0).then_inc(const_ready, 1)
            g.memset(ones_f[:, :], 1.0).then_inc(const_ready, 1)
            g.memset(ones_b[:, :], 1.0).then_inc(const_ready, 1)
            g.memset(to_row[:, :], 0.0).then_inc(const_ready, 1)
            pool.wait_ge(const_ready, 4)
            g.memset(to_row[:, CHUNKS - 1:CHUNKS], 1.0).then_inc(const_ready, 1)
            g.affine_select(out=before_f[:, :], in_=ones_f[:, :], compare_op=ALU.is_gt, fill=0.0,
                            base=0, pattern=[[1, P]], channel_multiplier=-1).then_inc(const_ready, 1)
            g.affine_select(out=ident[:, :], in_=ident[:, :], compare_op=ALU.not_equal, fill=1.0,
                            base=0, pattern=[[-1, P]], channel_multiplier=1).then_inc(const_ready, 1)
            g.affine_select(out=before[:, :], in_=ones_b[:, :], compare_op=ALU.is_gt, fill=0.0,
                            base=0, pattern=[[1, P]], channel_multiplier=-1).then_inc(const_ready, 1)
            g.iota(iota_p[:, :], pattern=[[1, P]], base=0, channel_multiplier=0,
                   allow_small_or_imprecise_dtypes=True).then_inc(const_ready, 1)
            g.iota(iota_run[:, :], pattern=[[1, RUNS * P]], base=0, channel_multiplier=0,
                   allow_small_or_imprecise_dtypes=True).then_inc(const_ready, 1)
            g.iota(iota_b[:, :], pattern=[[1, NB]], base=0, channel_multiplier=0,
                   allow_small_or_imprecise_dtypes=True).then_inc(const_ready, 1)
            g.iota(iota_w[:, :], pattern=[[1, BLK]], base=0, channel_multiplier=0,
                   allow_small_or_imprecise_dtypes=True).then_inc(const_ready, 1)
            g.iota(iota_t[:, :], pattern=[[1, TAB // P]], base=0, channel_multiplier=TAB // P,
                   allow_small_or_imprecise_dtypes=True).then_inc(const_ready, 1)

            pool.sem_inc(hist_done, HISTCREDIT)
            pool.sem_inc(x0_kept, 1)
            pool.sem_inc(part_ready, READYCREDIT)
            pool.sem_inc(part_added, ADDCREDIT)

            def taken_up():
                pool.sem_inc(pool_groups, 1)

            with pool.Fori(0, XOUT) as j:
                for q in range(XR):
                    pool.wait_ge(x0_idx, j * XR + (q + 1))
                    taken_up()
                    for k in range(q * XG, q * XG + XG):
                        pool.indirect_dma_start(
                            out=xg[0:HALF, k, :], out_offset=None, in_=emb,
                            in_offset=bass.IndirectOffsetOnAxis(ap=idx[0:HALF, k:k + 1], axis=0),
                        ).then_inc(x0_got[q], DMA)

            pool.wait_ge(zero_filled, 4 * DMA)

            def scatter(i, q, first):
                pool.wait_ge(stage_ready, i * 2 + (q + 1))
                if not (first and q == 0):
                    pool.wait_ge(scattered[1 - q], i * (RUNS * DMA) + q * (RUNS * DMA))
                taken_up()
                for k in range(RUNS):
                    pool.indirect_dma_start(
                        out=sorted_edges,
                        out_offset=bass.IndirectOffsetOnAxis(ap=run_idx[:, q, k:k + 1], axis=0),
                        in_=stage[:, q, k * RUN:(k + 1) * RUN, :].rearrange("p c f -> p (c f)"), in_offset=None,
                        compute_op=ALU.add,
                    ).then_inc(scattered[q], DMA)

            for q in range(2):
                scatter(0, q, True)
            with pool.Fori(1, PAIRS) as i:
                for q in range(2):
                    scatter(i, q, False)
            scatter(PAIRS, 0, False)

            for q in range(XR):
                pool.wait_ge(x0_stored[q], XOUT * 2 * DMA)
            with pool.Fori(0, LAYERS) as la:
                with pool.Fori(0, STEPS) as i:
                    for gr in range(RING):
                        pool.wait_ge(idx_ready, la * GROUPS + i * RING + (gr + 1))
                        taken_up()
                        for k in range(gr * GRP, gr * GRP + GRP):
                            pool.indirect_dma_start(
                                out=xg[:, k, :], out_offset=None, in_=x_now,
                                in_offset=bass.IndirectOffsetOnAxis(ap=idx[:, k:k + 1], axis=0),
                            ).then_inc(gathered[gr], DMA)
                pool.wait_ge(part_added, ADDCREDIT + la * TILES + TILES)
                pool.wait_ge(part_ready, READYCREDIT + la * GROUPS + GROUPS)

                def dense_pair(j, first):
                    for q in range(2):
                        if not first:
                            pool.wait_ge(z_ready, la * NB + j * 2 + (q - 1))
                        blk = bass.ds(j * (2 * BLK) + q * BLK, BLK)
                        g.tensor_tensor(prodT[q], hT[:, blk], xT[:, blk], ALU.mult).then_inc(prod_ready, 1)

                dense_pair(0, True)
                with pool.Fori(1, NB // 2) as j:
                    dense_pair(j, False)
                for q in range(2):
                    pool.wait_ge(stored[q], la * (NB * DMA) + NB * DMA)

        @block.sync
        def _(sp):
            for k, src in enumerate((row, col, vals)):
                dst = (raw_row, raw_col, raw_val)[k]
                sp.dma_start(dst, src.rearrange("(p c) -> p c", p=P)).then_inc(edges_in, DMA)
            sp.dma_start(ids_c[:, :], ids.rearrange("(c r) -> c r", r=HALF)).then_inc(ids_in, DMA)
            for k, w in enumerate(weights):
                sp.dma_start(w_raw[:, k, :], w).then_inc(w_in, DMA)
            for k, b in enumerate(biases):
                sp.dma_start(bias[0:1, 1 + k % 2, k // 2, :], b.rearrange("(a d) -> a d", a=1)).then_inc(w_in, DMA)
            sp.wait_ge(zeros_ready, 1)
            fill = sorted_edges.rearrange("(p t) c -> p (t c)", p=P)
            for k in range(4):
                sp.dma_start(fill[:, k * ZW:(k + 1) * ZW], zeros[:, 0:ZW]).then_inc(zero_filled, DMA)

            x0_out = out.rearrange("(n k r) f -> n r k f", k=XG, r=HALF)
            x0_now = x_now.rearrange("(n k r) f -> n r k f", k=XG, r=HALF)
            with sp.Fori(0, XOUT) as j:
                for q in range(XR):
                    sp.wait_ge(x0_got[q], j * (XG * DMA) + XG * DMA)
                    sp.dma_start(x0_out[bass.ds(j * XR + q, 1), :, :, 0:D].rearrange("a r k f -> (a r) k f"),
                                 xg[0:HALF, q * XG:q * XG + XG, :]).then_inc(x0_stored[q], DMA)
                    sp.dma_start(x0_now[bass.ds(j * XR + q, 1), :, :, :].rearrange("a r k f -> (a r) k f"),
                                 xg[0:HALF, q * XG:q * XG + XG, :]).then_inc(x0_stored[q], DMA)

            sp.wait_ge(places_ready, 1)
            for k in range(2):
                sp.dma_start(chunk_places[k, :].rearrange("(c b) -> c b", b=NB), places_hl[:, k, :]).then_inc(places_stored, DMA)
            sp.wait_ge(places_stored, 2 * DMA)
            sp.dma_start(places, chunk_places).then_inc(places_in, DMA)
            sp.wait_ge(tab_ready, 1)
            sp.dma_start(tile_offsets, tab_i[:, :]).then_inc(tab_stored, DMA)
            sp.wait_ge(tab_stored, DMA)
            sp.wait_ge(scattered[0], (PAIRS + 1) * RUNS * DMA)
            sp.wait_ge(scattered[1], PAIRS * RUNS * DMA)
            sp.dma_start(unsorted.rearrange("p g l f -> p (g l f)"),
                         sorted_edges[0:DUMP, :].rearrange("(p t) c -> p (t c)", p=P)).then_inc(recs_in, DMA)
            sp.dma_start(table, tile_offsets.rearrange("p t -> (p t)").rearrange("(a t) -> a t", a=1)).then_inc(tab_in, DMA)

            new_out = out.rearrange("(n h r) (l d) -> n l r h d", h=2, r=HALF, d=D)
            new_now = x_now.rearrange("(n h r) d -> n r h d", h=2, r=HALF)
            with sp.Fori(0, LAYERS) as la:
                with sp.Fori(0, NB // 2) as j:
                    for q in range(2):
                        sp.wait_ge(new_ready, la * NB + j * 2 + (q + 1))
                        sp.dma_start(
                            new_out[bass.ds(j * 2 + q, 1), bass.ds(la + 1, 1), :, :, :].rearrange("a b r h d -> (a b r) h d"),
                            x_new[q]).then_inc(stored[q], DMA)
                        sp.dma_start(new_now[bass.ds(j * 2 + q, 1), :, :, :].rearrange("a r h d -> (a r) h d"),
                                     x_new[q]).then_inc(stored[q], DMA)
            for q in range(2):
                sp.wait_ge(stored[q], LAYERS * (NB // 2) * 2 * DMA)

        @block.scalar
        def _(act):
            s = nc.scalar
            act.wait_ge(const_ready, CONSTS)
            act.wait_ge(ids_ready, 1)

            def x0_index(col0, q):
                s.activation(idx[0:HALF, q * XG:q * XG + XG], ids_t[:, col0], ACT.Copy).then_inc(x0_idx, 1)

            def x0_keep(n, count):
                act.wait_ge(x0_turned, count)
                s.activation(xT[:, bass.ds(n * (XG * HALF), XG * HALF)], ps[:, 3, 0:XG * HALF], ACT.Copy).then_inc(x0_kept, 1)

            for n in range(XR - 1):
                x0_index(slice(n * XG, n * XG + XG), n)
            x0_keep(0, 1)
            x0_index(slice((XR - 1) * XG, XR * XG), XR - 1)
            with act.Fori(0, XOUT - 1) as j:
                for q in range(XR):
                    x0_keep(j * XR + (q + 1), j * XR + (q + 2))
                    act.wait_ge(x0_stored[q], j * (2 * DMA) + 2 * DMA)
                    x0_index(bass.ds(j * (XR * XG) + (XR + q) * XG, XG), q)
            for n in range(XGROUPS - XR + 1, XGROUPS):
                x0_keep(n, n + 1)

            act.wait_ge(run_tab_ready, 1)

            def stage_chunk(i, q, first):
                if not first:
                    act.wait_ge(scattered[q], i * (RUNS * DMA))
                s.activation(run_idx[:, q, :], run_tab[:, :, bass.ds(i * 2 + q, 1)].rearrange("p k a -> p (k a)"), ACT.Copy)
                act.wait_ge(ordered, i * 2 + (q + 1))
                s.activation(stage[:, q, :, :], ps[:, 6 + q, 0:2 * SLOTS].rearrange("p (f c) -> p c f", f=2),
                             ACT.Copy).then_inc(stage_ready, 1)

            for q in range(2):
                stage_chunk(0, q, True)
            with act.Fori(1, PAIRS) as i:
                for q in range(2):
                    stage_chunk(i, q, False)
            stage_chunk(PAIRS, 0, False)

            keep_turned(act, s.activation, 1, ACT.Copy)
            act.wait_ge(col_ready, 1)
            with act.Fori(0, LAYERS) as la:
                with act.Fori(0, STEPS) as i:
                    for gr in range(RING):
                        act.wait_ge(part_ready, la * GROUPS + i * RING + (gr + 1))
                        s.activation(idx[:, gr * GRP:gr * GRP + GRP], recs[:, 0, bass.ds(i * STEP + gr * GRP, GRP)],
                                     ACT.Copy).then_inc(idx_ready, 1)

                def dense_pair(j, first):
                    n = la * NB + j * 2
                    for q in range(2):
                        act.wait_ge(z_ready, n + (q + 1))
                        if not first:
                            act.wait_ge(new_ready, n + (q - 1))
                        s.activation(low[q], zps[q], ACT.Copy, scale=SLOPE).then_inc(low_ready, 1)
                    if first:
                        act.wait_ge(zconst_ready, la + 1)
                    for q in range(2):
                        blk = bass.ds(j * (2 * BLK) + q * BLK, BLK)
                        s.activation(hT[:, blk], zero_blk, ACT.Copy).then_inc(blk_zeroed, 1)
                    for q in range(2):
                        blk = bass.ds(j * (2 * BLK) + q * BLK, BLK)
                        act.wait_ge(new_turned, n + (q + 1))
                        s.activation(xT[:, blk], tps[q], ACT.Copy).then_inc(xT_ready, 1)

                dense_pair(0, True)
                with act.Fori(1, NB // 2) as j:
                    dense_pair(j, False)

        @block.tensor
        def _(pe):
            t = nc.tensor
            pe.wait_ge(const_ready, CONSTS)
            pe.wait_ge(w_in, 4 * LAYERS * DMA)
            for k in range(2 * LAYERS):
                last = t.transpose(ps[:, 5 + k // 4, (k % 4) * D:(k % 4 + 1) * D], w_raw[:, k, :], ident[:, :])
            last.then_inc(w_turned, 1)
            pe.wait_ge(ids_float, 1)
            t.transpose(ps[0:HALF, 7, 0:N // HALF], ids_f[:, :], ident[0:N // HALF, 0:N // HALF]).then_inc(ids_turned, 1)

            pe.wait_ge(zeros_ready, 1)
            zb = zeros.bitcast(BF16)
            for a, lanes in LANE_BANKS:
                t.matmul(acc[:, a, 0:lanes * NB], to_row[:, 0:CHUNKS], zb[:, 0:lanes * NB], start=True, stop=True)

            def hist(it, r):
                pe.wait_ge(onehot_ready, it + 1)
                for a, lanes in LANE_BANKS:
                    last = t.matmul(acc[:, a, 0:lanes * NB], to_row[:, bass.ds(it * -1 + (CHUNKS - 1), CHUNKS)],
                                    oh[:, r, a * BANKL:a * BANKL + lanes, :].rearrange("p l b -> p (l b)"),
                                    start=False, stop=True, skip_group_check=True)
                last.then_inc(hist_done, 1)

            with pe.Fori(0, XOUT) as j:
                for q in range(XR):
                    for r in range(SR):
                        hist(j * (XR * SR) + (q * SR + r), r)
                    pe.wait_ge(x0_got[q], j * (XG * DMA) + XG * DMA)
                    pe.wait_ge(x0_kept, j * XR + (q + 1))
                    for k in range(XG):
                        last = t.transpose(ps[:, 3, k * HALF:(k + 1) * HALF], xg[0:HALF, q * XG + k, :], ident[0:HALF, 0:HALF])
                    last.then_inc(x0_turned, 1)

            pe.wait_ge(counts_ready, 1)
            t.matmul(ps[:, 4, 0:NB], ones_f[0:CHUNKS, :], small[0:CHUNKS, 0, 0:NB], start=True, stop=True)
            t.matmul(ps[0:CHUNKS, 5, 0:NB], before_f[0:CHUNKS, 0:CHUNKS], small[0:CHUNKS, 0, 0:NB],
                     start=True, stop=True).then_inc(sums_ready, 1)
            pe.wait_ge(run_to_ready, 1)
            for k in range(RUNS):
                last = t.transpose(ps[:, 7, k * CHUNKS:(k + 1) * CHUNKS],
                                   run_to.rearrange("c (p k) -> c k p", k=RUNS)[:, k, :], ident[0:CHUNKS, 0:CHUNKS])
            last.then_inc(run_turned, 1)
            pe.wait_ge(places_in, DMA)
            pe.wait_ge(x0_kept, XGROUPS + 1)

            def rank(i, q, first):
                n = i * 2 + q
                pe.wait_ge(onehot2_ready, n + 1)
                if not first:
                    pe.wait_ge(rank_read, n - 1)
                mm = lambda a, l0, l1, lhs, rhs, **kw: t.matmul(
                    ps[:, 3 * q + a, (l0 - a * BANKL) * NB:(l1 - a * BANKL) * NB], lhs, rhs, skip_group_check=True, **kw)
                spread = lambda src, k: src[:, None, :].to_broadcast([src.shape[0], k, NB])
                for a, lanes in LANE_BANKS:
                    l0, l1 = a * BANKL, a * BANKL + lanes
                    mm(a, l0, l1, ones_b[0:2, :], spread(places[:, bass.ds(n * NB, NB)], lanes), start=True, stop=False)
                    mm(a, l0, l1, before[:, :], oh[:, q, l0:l1, :].rearrange("p l b -> p (l b)"), start=False, stop=False)
                    if a:
                        mm(a, l0, l1, ones_b[:, :], spread(first10[:, q, :], lanes), start=False, stop=False)
                    for src in range(BANKL if a else 0, l1 - 1):
                        to = max(l0, src + 1)
                        last = mm(a, to, l1, ones_b[:, :], spread(oh[:, q, src, :], l1 - to), start=False, stop=src == l1 - 2)
                last.then_inc(rank_ready, 1)

            def order(i, q, first):
                n = i * 2 + q
                pe.wait_ge(moved_ready, n + 1)
                if not first:
                    pe.wait_ge(stage_ready, n - 1)
                for k in range(LANES):
                    last = t.matmul(ps[:, 6 + q, 0:2 * SLOTS], to_part[q][:, k, :],
                                    moved[q][:, k, :, :].rearrange("p f c -> p (f c)"), start=k == 0, stop=k == LANES - 1)
                last.then_inc(ordered, 1)

            rank(0, 0, True)
            rank(0, 1, True)
            order(0, 0, True)
            rank(1, 0, False)
            order(0, 1, True)
            with pe.Fori(1, PAIRS) as i:
                rank(i, 1, False)
                order(i, 0, False)
                rank(i + 1, 0, False)
                order(i, 1, False)
            order(PAIRS, 0, False)

            pe.wait_ge(recs_in, DMA)
            for m, (f, g0, g1) in enumerate(TURNS):
                if m >= 8:
                    pe.wait_ge(turned_kept[f], (m - 8) // 2 + 1)
                for k in range(g0, g1):
                    last = t.transpose(ps[:, m % 8, (k - g0) * P:(k - g0 + 1) * P], unsorted[:, k, :, f], ident[:, :])
                last.then_inc(turned, 1)

            pe.wait_ge(w_ready, 1)
            with pe.Fori(0, LAYERS) as la:
                with pe.Fori(0, STEPS) as i:
                    for gr in range(RING):
                        n = la * GROUPS + i * RING
                        pe.wait_ge(gathered[gr], la * (STEPS * GRP * DMA) + i * (GRP * DMA) + GRP * DMA)
                        pe.wait_ge(sel_ready, n + (gr + 1))
                        pe.wait_ge(part_added, la * TILES + i * STEP + (gr + 1) * GRP)
                        for k in range(GRP):
                            last = t.matmul(part[(gr % 2) * GRP + k], xg[:, gr * GRP + k, :],
                                            sel[:, (gr % 2) * GRP + k, :], start=True, stop=True)
                        last.then_inc(part_ready, 1)

                def dense_pair(j, first):
                    n = la * NB + j * 2
                    for q in range(2):
                        pe.wait_ge(sum_ready, n + (q + 1))
                        pe.wait_ge(prod_ready, n + (q + 1))
                        if not first:
                            pe.wait_ge(new_ready, n + (q - 1))
                        for h in range(2):
                            rows = slice(h * HALF, (h + 1) * HALF)
                            t.matmul(zps[q][:, h, :], sumT[q][:, rows], w_sb[:, bass.ds(la, 1), 0, :].rearrange("p a d -> p (a d)"), start=True, stop=False)
                            t.matmul(zps[q][:, h, :], prodT[q][:, rows], w_sb[:, bass.ds(la, 1), 1, :].rearrange("p a d -> p (a d)"), start=False, stop=False)
                            last = t.matmul(zps[q][:, h, :], ones_f[0:1, 0:HALF], bias[0:1, 0, bass.ds(la, 1), :].rearrange("p a d -> p (a d)"),
                                            start=False, stop=True)
                        last.then_inc(z_ready, 1)
                    for q in range(2):
                        pe.wait_ge(new_ready, n + (q + 1))
                        if not first:
                            pe.wait_ge(xT_ready, n + (q - 1))
                        for h in range(2):
                            last = t.transpose(tps[q][:, h * HALF:(h + 1) * HALF], x_new[q][:, h, :], ident[0:HALF, 0:HALF])
                        last.then_inc(new_turned, 1)

                dense_pair(0, True)
                with pe.Fori(1, NB // 2) as j:
                    dense_pair(j, False)

        @block.vector
        def _(dve):
            v = nc.vector
            links = [0]

            def link(ins):
                links[0] += 1
                ins.then_inc(dve_link, 1)
                dve.wait_ge(dve_link, links[0])

            v.memset(zeros, 0.0).then_inc(zeros_ready, 1)
            dve.wait_ge(ids_in, DMA)
            v.tensor_copy(ids_f[:, :], ids_c[:, :]).then_inc(ids_float, 1)
            dve.wait_ge(ids_turned, 1)
            v.tensor_copy(ids_t[:, :], ps[0:HALF, 7, 0:N // HALF]).then_inc(ids_ready, 1)

            dve.wait_ge(edges_in, 3 * DMA)
            exact = hT[:, OP0:OP0 + COLS]
            link(v.tensor_scalar(exact, raw_row, -(BLK - 1) / 2, 1.0 / BLK, ALU.add, ALU.mult))
            link(v.tensor_scalar(block_of, exact, ROUND, -ROUND, ALU.add, ALU.add))
            link(v.scalar_tensor_tensor(packed, block_of, -float(BLK), raw_row, ALU.mult, ALU.add))
            v.scalar_tensor_tensor(packed, raw_col, PACK, packed, ALU.mult, ALU.add).then_inc(packed_ready, 1)

            dve.wait_ge(const_ready, CONSTS)

            def one_hot(it, r):
                return v.tensor_tensor(oh[:, r, :, :],
                                       block_of[:, bass.ds(it * LANES, LANES)][:, :, None].to_broadcast([P, LANES, NB]),
                                       iota_b[:, None, :].to_broadcast([P, LANES, NB]), ALU.is_equal)

            with dve.Fori(0, SOUT) as j:
                for r in range(SR):
                    dve.wait_ge(hist_done, j * SR + (r + 1))
                    one_hot(j * SR + r, r).then_inc(onehot_ready, 1)

            dve.wait_ge(w_turned, 1)
            wf = w_sb[:, :, :, :].rearrange("p l k d -> p (l k d)")
            v.tensor_copy(wf[:, 0:4 * D], ps[:, 5, 0:4 * D])
            v.tensor_copy(wf[:, 4 * D:6 * D], ps[:, 6, 0:2 * D])
            v.tensor_tensor(bias[0:1, 0, :, :], bias[0:1, 1, :, :], bias[0:1, 2, :, :], ALU.add).then_inc(w_ready, 1)

            names = "count sum_ before_ n_tiles end_tile ones cursor run0 phase n_runs end_run start_run at shift".split()
            of = {name: small[0:CHUNKS, k, 0:NB] for k, name in enumerate(names)}
            whole = {name: small[:, k, 0:NB] for k, name in enumerate(names)}
            dve.wait_ge(hist_done, CHUNKS + SR)
            v.tensor_copy(counts[:, :, 0:2 * BANKL].rearrange("p b (a l) -> p a l b", a=2),
                          acc[:, 0:2, 0:BANKL * NB].rearrange("p a (l b) -> p a l b", b=NB))
            link(v.tensor_copy(counts[:, :, 2 * BANKL:LANES].rearrange("p b l -> p l b"),
                               acc[:, 2, 0:(LANES - 2 * BANKL) * NB].rearrange("p (l b) -> p l b", b=NB)))
            v.memset(whole["ones"], 1.0)
            v.tensor_reduce(of["count"], counts, AX.X, ALU.add).then_inc(counts_ready, 1)
            dve.wait_ge(sums_ready, 1)
            link(v.tensor_scalar(whole["sum_"], ps[:, 4, 0:NB], (P - 1) / 2, 1.0 / P, ALU.add, ALU.mult))
            link(v.tensor_scalar(whole["n_tiles"], whole["sum_"], ROUND, -ROUND, ALU.add, ALU.add))
            link(v.tensor_tensor_scan(whole["end_tile"], whole["ones"], whole["n_tiles"], 0.0, ALU.mult, ALU.add))
            link(v.tensor_tensor(whole["at"], whole["end_tile"], whole["n_tiles"], ALU.subtract))
            link(v.scalar_tensor_tensor(of["cursor"], of["at"], float(P), ps[0:CHUNKS, 5, 0:NB], ALU.mult, ALU.add))
            link(v.tensor_scalar(of["before_"], of["cursor"], -(RUN - 1) / 2, 1.0 / RUN, ALU.add, ALU.mult))
            link(v.tensor_scalar(of["run0"], of["before_"], ROUND, -ROUND, ALU.add, ALU.add))
            link(v.scalar_tensor_tensor(of["phase"], of["run0"], -float(RUN), of["cursor"], ALU.mult, ALU.add))
            link(v.tensor_tensor(of["at"], of["phase"], of["count"], ALU.add))
            link(v.tensor_scalar(of["before_"], of["at"], (RUN - 1) / 2, 1.0 / RUN, ALU.add, ALU.mult))
            link(v.tensor_scalar(of["n_runs"], of["before_"], ROUND, -ROUND, ALU.add, ALU.add))
            link(v.tensor_tensor_scan(of["end_run"], of["ones"], of["n_runs"], 0.0, ALU.mult, ALU.add))
            link(v.tensor_tensor(of["start_run"], of["end_run"], of["n_runs"], ALU.subtract))
            link(v.scalar_tensor_tensor(of["at"], of["start_run"], float(RUN), of["phase"], ALU.mult, ALU.add))
            link(v.tensor_scalar(of["before_"], of["at"], -(QHI - 1) / 2, 1.0 / QHI, ALU.add, ALU.mult))
            link(v.tensor_scalar(of["cursor"], of["before_"], ROUND, -ROUND, ALU.add, ALU.add))
            v.tensor_scalar(places_hl[:, 0, :], of["cursor"], QHI, None, ALU.mult)
            v.scalar_tensor_tensor(places_hl[:, 1, :], of["cursor"], -QHI, of["at"],
                                   ALU.mult, ALU.add).then_inc(places_ready, 1)
            link(v.tensor_tensor(of["shift"], of["run0"], of["start_run"], ALU.subtract))
            step_at = small[0:CHUNKS, names.index("start_run"), :]
            step_by = small[0:CHUNKS, names.index("sum_"), :]
            v.tensor_copy(step_at[:, NB:NB + 1], of["end_run"][:, NB - 1:NB])
            v.tensor_copy(step_by[:, 0:1], of["shift"][:, 0:1])
            v.tensor_tensor(step_by[:, 1:NB], of["shift"][:, 1:NB], of["shift"][:, 0:NB - 1], ALU.subtract)
            v.tensor_scalar(step_by[:, NB:NB + 1], of["shift"][:, NB - 1:NB], -1.0, float(DUMP), ALU.mult, ALU.add)
            link(v.tensor_copy(run_to, iota_run[0:CHUNKS, :]))
            with dve.Fori(0, NB + 1) as b:
                v.tensor_scalar(run_add, iota_run[0:CHUNKS, :], step_at[:, bass.ds(b, 1)], step_by[:, bass.ds(b, 1)],
                                ALU.is_ge, ALU.mult).then_inc(run_link, 1)
                dve.wait_ge(run_link, b * 2 + 1)
                v.tensor_tensor(run_to, run_to, run_add, ALU.add).then_inc(run_link, 1)
                dve.wait_ge(run_link, b * 2 + 2)
            v.engine_nop().then_inc(run_to_ready, 1)
            big = ranked[:, :].rearrange("p (t b) -> p t b", b=NB)
            link(v.tensor_tensor(big, iota_t[:, :, None].to_broadcast([P, TABW, NB]),
                                 whole["end_tile"][:, None, :].to_broadcast([P, TABW, NB]), ALU.is_ge))
            link(v.tensor_reduce(tab_f[:, :], big, AX.X, ALU.add))
            v.tensor_scalar(tab_i[:, :], tab_f[:, :], float(NB - 1), float(BLK), ALU.min, ALU.mult).then_inc(tab_ready, 1)
            dve.wait_ge(run_turned, 1)
            v.tensor_copy(run_tab[:, :, :].rearrange("p k c -> p (k c)"), ps[:, 7, 0:RUNS * CHUNKS]).then_inc(run_tab_ready, 1)

            def one_hot_sum(n, q):
                one_hot(n, q).then_inc(sum_link, 1)
                dve.wait_ge(sum_link, n + 1)
                with nc.allow_low_precision(reason="counts up to ten are exact"):
                    v.tensor_reduce(first10[:, q, :], oh[:, q, 0:BANKL, :].rearrange("p l b -> p b l"),
                                    AX.X, ALU.add).then_inc(onehot2_ready, 1)

            def chunk(i, q, first, more):
                n = i * 2 + q
                links_of = [0]

                def chain(ins):
                    links_of[0] += 1
                    ins.then_inc(rank_link, 1)
                    dve.wait_ge(rank_link, n * 4 + links_of[0])

                if more:
                    one_hot_sum(n + 1, 1 - q)
                dve.wait_ge(rank_ready, n + 1)
                v.tensor_tensor(ranked[:, 0:2 * BANKL * NB].rearrange("p (a x) -> p a x", a=2),
                                ps[:, 3 * q:3 * q + 2, 0:BANKL * NB],
                                oh[:, q, 0:2 * BANKL, :].rearrange("p (a l) b -> p a (l b)", a=2), ALU.mult)
                v.tensor_tensor(ranked[:, 2 * BANKL * NB:OHW], ps[:, 3 * q + 2, 0:(LANES - 2 * BANKL) * NB],
                                oh[:, q, 2 * BANKL:LANES, :].rearrange("p l b -> p (l b)"), ALU.mult).then_inc(rank_read, 1)
                dve.wait_ge(rank_read, n + 1)
                chain(v.tensor_reduce(place[:, 0, :], ranked[:, :].rearrange("p (l b) -> p l b", b=NB), AX.X, ALU.add))
                chain(v.tensor_scalar(place[:, 1, :], place[:, 0, :], -(SLOTS - 1) / 2, 1.0 / SLOTS, ALU.add, ALU.mult))
                chain(v.tensor_scalar(place[:, 2, :], place[:, 1, :], ROUND, -ROUND, ALU.add, ALU.add))
                v.scalar_tensor_tensor(place[:, 3, :], place[:, 2, :], -float(SLOTS), place[:, 0, :],
                                       ALU.mult, ALU.add).then_inc(slot_link, 1)
                if not first:
                    dve.wait_ge(ordered, n - 1)
                v.tensor_tensor(to_part[q], place[:, 2, :][:, :, None].to_broadcast([P, LANES, P]),
                                iota_p[:, None, :].to_broadcast([P, LANES, P]), ALU.is_equal)
                dve.wait_ge(slot_link, n + 1)
                chain(v.tensor_tensor(in_slot, place[:, 3, :][:, :, None].to_broadcast([P, LANES, SLOTS]),
                                      iota_p[:, None, 0:SLOTS].to_broadcast([P, LANES, SLOTS]), ALU.is_equal))
                for f, field in enumerate((packed, raw_val)):
                    last = v.tensor_tensor(moved[q][:, :, f, :], in_slot,
                                           field[:, bass.ds(n * LANES, LANES)][:, :, None].to_broadcast([P, LANES, SLOTS]),
                                           ALU.mult)
                last.then_inc(moved_ready, 1)

            dve.wait_ge(zero_filled, 4 * DMA)
            dve.wait_ge(x0_kept, XGROUPS + 1)
            for q in range(XR):
                dve.wait_ge(x0_stored[q], XOUT * 2 * DMA)
            one_hot_sum(0, 0)
            for q in range(2):
                chunk(0, q, True, True)
            with dve.Fori(1, PAIRS) as i:
                for q in range(2):
                    chunk(i, q, False, True)
            chunk(PAIRS, 0, False, False)

            keep_turned(dve, v.tensor_copy, 0)
            dve.wait_ge(turned_kept[0], len(TURNS) // 2)
            link(v.tensor_scalar(recs[:, 1, :], recs[:, 0, :], -(PACK - 1) / 2, 1.0 / PACK, ALU.add, ALU.mult))
            link(v.tensor_scalar(recs[:, 1, :], recs[:, 1, :], ROUND, -ROUND, ALU.add, ALU.add))
            row_in = hT[:, 0:TAB]
            link(v.scalar_tensor_tensor(row_in, recs[:, 1, :], -PACK, recs[:, 0, :], ALU.mult, ALU.add))
            v.tensor_copy(recs[:, 0, :], recs[:, 1, :]).then_inc(col_ready, 1)
            dve.wait_ge(col_ready, 1)
            link(v.tensor_copy(recs[:, 1, :], row_in))
            dve.wait_ge(turned_kept[1], len(TURNS) // 2)
            link(v.memset(hT[:, :], 0.0))
            dve.wait_ge(tab_in, DMA)
            with dve.Fori(0, LAYERS) as la:
                def select(t0, gr, k):
                    slot = (gr % 2) * GRP + k
                    at = bass.ds(t0 + (gr * GRP + k), 1)
                    return v.tensor_scalar(sel[:, slot, :], iota_w[:, :], recs[:, 1, at], recs[:, 2, at],
                                           ALU.is_equal, ALU.mult)

                def step(t0, i, last_step):
                    for gr in range(RING):
                        _, offs = nc.values_load_multi_w_load_instructions(
                            table[0:1, bass.ds(t0 + gr * GRP, GRP)], engines=[mybir.EngineType.DVE],
                            min_val=0, max_val=N - BLK, skip_runtime_bounds_check_because="the table holds offsets of blocks")
                        dve.wait_ge(part_ready, la * GROUPS + i * RING + (READYCREDIT + gr + 1))
                        for k in range(GRP):
                            dve.wait_ge(part_added, la * TILES + i * STEP + (ADDCREDIT + gr * GRP + k))
                            blk = hT[:, bass.ds(offs[k], BLK)]
                            v.tensor_tensor(blk, blk, part[(gr % 2) * GRP + k], ALU.add).then_inc(part_added, 1)
                            if not (last_step and gr >= RING - 2):
                                built = select(t0, gr + 2, k)
                                if k == GRP - 1:
                                    built.then_inc(sel_ready, 1)

                for gr in range(2):
                    for k in range(GRP):
                        built = select(0, gr, k)
                    built.then_inc(sel_ready, 1)
                with dve.Fori(0, STEPS - 1) as i:
                    step(i * STEP, i, False)
                step((STEPS - 1) * STEP, STEPS - 1, True)

                dve.wait_ge(part_added, la * TILES + (ADDCREDIT + TILES))
                v.memset(zero_blk, 0.0).then_inc(zconst_ready, 1)

                def dense_pair(j, first):
                    n = la * NB + j * 2
                    for q in range(2):
                        blk = bass.ds(j * (2 * BLK) + q * BLK, BLK)
                        if not first:
                            dve.wait_ge(z_ready, n + (q - 1))
                        v.tensor_tensor(sumT[q], hT[:, blk], xT[:, blk], ALU.add).then_inc(sum_ready, 1)
                    for q in range(2):
                        dve.wait_ge(low_ready, n + (q + 1))
                        if not first:
                            dve.wait_ge(new_turned, n + (q - 1))
                            dve.wait_ge(stored[q], la * (NB * DMA) + j * (2 * DMA))
                        v.tensor_tensor(x_new[q], zps[q], low[q], ALU.max).then_inc(new_ready, 1)

                dense_pair(0, True)
                with dve.Fori(1, NB // 2) as j:
                    dense_pair(j, False)
                dve.wait_ge(blk_zeroed, la * NB + NB)


_INS = ["r_x_ids", "L0_rec_row", "L0_rec_col", "L0_rec_vals", "L0_rec_emb"]
_LAYERS = [("L0_rec_W%d_%d" % (la, k), "L0_rec_b%d_%d" % (la, k)) for la in (1, 2, 3) for k in (1, 2)]


def kernel(**inputs):
    import numpy as np
    import concourse.bacc as bacc
    from concourse.bass_utils import run_bass_kernel_spmd

    nc = bacc.Bacc("TRN2", target_bir_lowering=False, num_devices=1)
    arrays, aps = {}, {}
    for name in _INS + [n for pair in _LAYERS for n in pair]:
        a = np.ascontiguousarray(inputs[name])
        arrays["in_" + name] = a
        aps[name] = nc.dram_tensor("in_" + name, a.shape, mybir.dt.from_np(a.dtype), kind="ExternalInput").ap()
    out = nc.dram_tensor("out_x", (N, D * (LAYERS + 1)), F32, kind="ExternalOutput").ap()
    graph_layers(nc, *[aps[n] for n in _INS], [aps[w] for w, _ in _LAYERS], [aps[b] for _, b in _LAYERS], out)
    r = run_bass_kernel_spmd(nc, [arrays], core_ids=[0])
    return r.results[0]["out_x"]
```

```python
from contextlib import ExitStack

import concourse.bass as bass
from concourse import mybir

F32 = mybir.dt.float32
BF16 = mybir.dt.bfloat16
I32 = mybir.dt.int32
ALU = mybir.AluOpType
ACT = mybir.ActivationFunctionType
AX = mybir.AxisListType

P = 128
N = 12500
E = 400000
D = 128
LAYERS = 3
SLOPE = 0.2
DMA = 16

BLK = 250
NB = N // BLK
HALF = BLK // 2
COLS = E // P
GRP = 5
RING = 4
STEP = GRP * RING
TILES = -(-(COLS + NB) // STEP) * STEP
STEPS = TILES // STEP
GROUPS = TILES // GRP

LANES = 25
CHUNKS = COLS // LANES
BANKL = 10
SUMMED = 5
SR = 5
STR = 3
assert NB % SR == 0 and (NB + 1) % STR == 0
PAIRS = CHUNKS // 2
OHW = LANES * NB
TABW = -(-TILES // P)
TAB = TABW * P
RUN = 8
RUNS = 4
SLOTS = RUN * RUNS
assert LANES * P + NB * 2 * (RUN - 1) <= P * SLOTS
DUNROLL = 10
XNEW = 5
DUMP = TAB * P // RUN
PACK = 256.0
QHI = 16.0
OPW = LANES * P
ACTL = 19

XG = 4
XGROUPS = N // (HALF * XG)
XR = RING * GRP // XG
XOUT = XGROUPS // XR
HX = NB // XGROUPS
assert NB % XGROUPS == 0 and (XR * HX) % SR == 0

ROUND = 12582912.0


def graph_layers(nc, ids, row, col, vals, emb, weights, biases, out):
    ctx = ExitStack()
    with ctx:
        def sb(name, shape, dt=F32):
            return ctx.enter_context(nc.sbuf_tensor(name, shape, dt))

        def sem(name):
            return ctx.enter_context(nc.semaphore(name))

        sorted_edges = nc.dram_tensor("sorted_edges", [DUMP + RUNS * P, RUN * 2], F32, kind="Internal").ap()
        chunk_places = nc.dram_tensor("chunk_places", [2, CHUNKS * NB], BF16, kind="Internal").ap()
        x_now = nc.dram_tensor("x_now", [N, D], F32, kind="Internal").ap()
        tile_offsets = nc.dram_tensor("tile_offsets", [P, TAB // P], I32, kind="Internal").ap()

        hT = sb("hT", [P, N])
        xT = sb("xT", [P, N])
        recs = sb("recs", [P, 3, TAB])
        xg = sb("xg", [P, RING * GRP, D])
        sel = sb("sel", [P, 2 * GRP, BLK])
        oh_tab = sb("oh_tab", [P, TAB])
        ranked = sb("ranked", [P, OHW])
        idx = sb("idx", [P, RING * GRP], I32)
        run_idx = sb("run_idx", [P, 2, RUNS], I32)
        run_tab = sb("run_tab", [P, RUNS, CHUNKS])
        place = sb("place", [P, 2, 4, LANES])
        stage = sb("stage", [P, 2, SLOTS, 2])
        sums = sb("sums", [P, 2, LANES // SUMMED - 1, NB], BF16)
        w_sb = sb("w_sb", [P, LAYERS, 2, D])
        bias = sb("bias", [P, 3, LAYERS])
        b_now = sb("b_now", [P, 1])
        w_now = sb("w_now", [P, 2, D])
        iota_w = sb("iota_w", [P, BLK])
        iota_b = sb("iota_b", [P, NB])
        iota_p = sb("iota_p", [P, P])
        iota_run = sb("iota_run", [P, RUNS * P])
        iota_t = sb("iota_t", [P, TAB // P])
        iota_pk = sb("iota_pk", [P, RUNS])
        ident = sb("ident", [P, P])
        ones_f = sb("ones_f", [P, P])
        before_f = sb("before_f", [P, P])
        ones_b = sb("ones_b", [P, P], BF16)
        ident_b = sb("ident_b", [P, P], BF16)
        before = sb("before", [P, P], BF16)
        ids_c = sb("ids_c", [N // HALF, HALF], I32)
        ids_f = sb("ids_f", [N // HALF, HALF])
        ids_t = sb("ids_t", [HALF, N // HALF])
        small = sb("small", [P, 16, NB + 1])
        tab_f = sb("tab_f", [P, TAB // P])
        tab_i = sb("tab_i", [P, TAB // P], I32)
        places_hl = sb("places_hl", [CHUNKS, 2, NB], BF16)
        ps = ctx.enter_context(nc.psum_tensor("ps", [P, 8, 512], F32))

        flat = recs[:, :, :].rearrange("p c t -> p (c t)")
        raw_row = flat[:, 0:COLS].bitcast(I32)
        raw_col = flat[:, COLS:2 * COLS].bitcast(I32)
        raw_val = flat[:, 2 * COLS:3 * COLS]
        packed = flat[:, 0:COLS]
        hb = hT[:, :].bitcast(BF16)
        block_of = hb[:, 0:COLS]
        OP0 = (COLS + 1) // 2
        to_part = [hT[:, OP0 + q * OPW:OP0 + (q + 1) * OPW].rearrange("p (l m) -> p l m", m=P) for q in range(2)]
        QB0 = OP0 + 2 * OPW
        places = hb[0:2, 2 * QB0:2 * QB0 + CHUNKS * NB]
        W0 = QB0 + (CHUNKS * NB + 1) // 2
        assert W0 + 6 * D <= N
        w_raw = hT[:, W0:W0 + 6 * D].rearrange("p (w d) -> p w d", d=D)
        FLAGW = OPW // 2
        assert 2 * FLAGW >= COLS
        ohb = oh_tab[:, :].bitcast(BF16)
        in_block = [hb[:, 2 * (OP0 + k * FLAGW):2 * (OP0 + k * FLAGW) + COLS] for k in range(4)] + [ohb[:, 0:COLS]]
        STEP0 = 2 * (OP0 + OPW)
        STEPW = RUNS * P + 2 * CHUNKS
        run_step = [hb[0:CHUNKS, STEP0 + r * STEPW:STEP0 + r * STEPW + RUNS * P] for r in range(STR)]
        run_diag = [hb[0:CHUNKS, STEP0 + r * STEPW + RUNS * P:STEP0 + (r + 1) * STEPW].rearrange("c (h m) -> c h m", h=2)
                    for r in range(STR)]
        assert STR * STEPW <= 2 * OPW
        unsorted = hT[:, 0:TABW * P * 2].rearrange("p (g l f) -> p g l f", l=P, f=2)
        zeros = sel[:, :, :].rearrange("p s w -> p (s w)")
        ZW = (DUMP + RUNS * P) * RUN * 2 // P // 4
        assert ZW <= 2 * GRP * BLK
        oh = ohb[:, 0:2 * OHW].rearrange("p (r l b) -> p r l b", r=2, b=NB)
        SLOTW = LANES * SLOTS
        in_slot = [oh_tab[:, OHW + q * SLOTW:OHW + (q + 1) * SLOTW].rearrange("p (l c) -> p l c", c=SLOTS) for q in range(2)]
        assert OHW + 2 * SLOTW <= TAB
        moved = [m[:, 0:2 * SLOTW].rearrange("p (l f c) -> p l f c", f=2, c=SLOTS)
                 for m in (zeros, xg[:, :, :].rearrange("p s d -> p (s d)"))]
        table = oh_tab[0:1, :].bitcast(I32)
        sumT = [sel[:, 0, :], sel[:, 1, :]]
        prodT = [sel[:, 2, :], sel[:, 3, :]]
        zero_blk = sel[:, 4, :]
        biased = [sel[:, 5, :], sel[:, 6, :]]
        newT = [sel[:, 7, :], sel[:, 8, :]]
        x_new = [xg[0:HALF, 2 * r:2 * r + 2, :] for r in range(XNEW)]

        acc = ps[0:CHUNKS, 2, 0:NB]
        part = [ps[:, 3 * g + k // 2, BLK * (k % 2):BLK * (k % 2 + 1)] for g in range(2) for k in range(GRP)]
        zps = [ps[:, q, 0:BLK] for q in range(2)]
        tps = [ps[0:HALF, 2 + q, 0:2 * D].rearrange("p (h d) -> p h d", h=2) for q in range(2)]
        LANE_BANKS = [(0, BANKL), (1, BANKL), (2, LANES - 2 * BANKL)]


        const_ready = sem("const_ready")
        edges_in = sem("edges_in")
        ids_in = sem("ids_in")
        w_in = sem("w_in")
        zero_filled = sem("zero_filled")
        zeros_ready = sem("zeros_ready")
        dve_link = sem("dve_link")
        slot_link = sem("slot_link")
        at_link = sem("at_link")
        raised_link = sem("raised_link")
        sum_link = sem("sum_link")
        ids_float = sem("ids_float")
        ids_turned = sem("ids_turned")
        ids_ready = sem("ids_ready")
        w_turned = sem("w_turned")
        w_ready = sem("w_ready")
        packed_ready = sem("packed_ready")
        onehot_ready = sem("onehot_ready")
        hist_done = sem("hist_done")
        counts_ready = sem("counts_ready")
        sums_ready = sem("sums_ready")
        places_ready = sem("places_ready")
        places_stored = sem("places_stored")
        places_in = sem("places_in")
        steps_ready = sem("steps_ready")
        steps_used = sem("steps_used")
        run_tab_ready = sem("run_tab_ready")
        onehot2_ready = sem("onehot2_ready")
        rank_ready = sem("rank_ready")
        rank_read = sem("rank_read")
        part_found = sem("part_found")
        parts_link = sem("parts_link")
        parts_ready = sem("parts_ready")
        in_slot_ready = sem("in_slot_ready")
        moved_ready = sem("moved_ready")
        vals_moved = sem("vals_moved")
        ordered = sem("ordered")
        stage_ready = sem("stage_ready")
        scattered = [sem(f"scattered{q}") for q in range(2)]
        turned = sem("turned")
        turned_kept = [sem(f"turned_kept{f}") for f in range(2)]
        col_ready = sem("col_ready")
        tab_ready = sem("tab_ready")
        tab_stored = sem("tab_stored")
        tab_in = sem("tab_in")
        recs_in = sem("recs_in")
        x0_idx = sem("x0_idx")
        x0_got = [sem(f"x0_got{q}") for q in range(XR)]
        x0_turned = sem("x0_turned")
        x0_kept = sem("x0_kept")
        x0_stored = [sem(f"x0_stored{q}") for q in range(XR)]
        idx_ready = sem("idx_ready")
        pool_groups = sem("pool_groups")
        act_copies = sem("act_copies")
        gathered = [sem(f"gathered{g}") for g in range(RING)]
        sel_ready = sem("sel_ready")
        part_ready = sem("part_ready")
        part_added = sem("part_added")
        sum_ready = sem("sum_ready")
        prod_ready = sem("prod_ready")
        blk_zeroed = sem("blk_zeroed")
        zconst_ready = sem("zconst_ready")
        z_ready = sem("z_ready")
        w_now_ready = sem("w_now_ready")
        biased_ready = sem("biased_ready")
        rows_ready = sem("rows_ready")
        new_ready = sem("new_ready")
        new_turned = sem("new_turned")
        xT_ready = sem("xT_ready")
        stored = [sem(f"stored{r}") for r in range(XNEW)]

        CONSTS = 12
        HISTCREDIT = SR
        STEPCREDIT = STR
        READYCREDIT = RING
        ADDCREDIT = 2 * GRP
        STORES = NB // XNEW * 2 * DMA

        TURNS = [(f, g0, min(g0 + 4, TABW)) for g0 in range(0, TABW, 4) for f in range(2)]

        def keep_turned(eng, copy, field, *how):
            rows = recs[:, 2 * field, :].rearrange("p (t g) -> p g t", g=TABW)
            for m, (f, g0, g1) in enumerate(TURNS):
                if f == field:
                    eng.wait_ge(turned, m + 1)
                    copy(rows[:, g0:g1, :], ps[:, m % 8, 0:(g1 - g0) * P].rearrange("p (g t) -> p g t", t=P),
                         *how).then_inc(turned_kept[f], 1)

        def all_blocks(eng, step):
            for k in range(DUNROLL):
                step(0, k, k)
            with eng.Fori(1, NB // DUNROLL - 1) as i:
                for k in range(DUNROLL):
                    step(i, k, None)
            for k in range(DUNROLL):
                step(NB // DUNROLL - 1, k, NB - DUNROLL + k)

        def block_before(i, k):
            return (i, k - 1) if k else (i - 1, DUNROLL - 1)

        last_block = (NB // DUNROLL - 1, DUNROLL - 1)

        def columns(i, k):
            return bass.ds(i * (DUNROLL * BLK) + k * BLK, BLK)

        def after(b, k):
            return b is None or b >= k

        block = ctx.enter_context(nc.Block())

        @block.gpsimd
        def _(pool):
            g = nc.gpsimd
            g.memset(ident[:, :], 0.0).then_inc(const_ready, 1)
            g.memset(ones_f[:, :], 1.0).then_inc(const_ready, 1)
            g.memset(ones_b[:, :], 1.0).then_inc(const_ready, 1)
            pool.wait_ge(const_ready, 3)
            g.affine_select(out=before_f[:, :], in_=ones_f[:, :], compare_op=ALU.is_gt, fill=0.0,
                            base=0, pattern=[[1, P]], channel_multiplier=-1).then_inc(const_ready, 1)
            g.affine_select(out=ident[:, :], in_=ident[:, :], compare_op=ALU.not_equal, fill=1.0,
                            base=0, pattern=[[-1, P]], channel_multiplier=1).then_inc(const_ready, 1)
            g.affine_select(out=before[:, :], in_=ones_b[:, :], compare_op=ALU.is_gt, fill=0.0,
                            base=0, pattern=[[1, P]], channel_multiplier=-1).then_inc(const_ready, 1)
            g.iota(iota_p[:, :], pattern=[[1, P]], base=0, channel_multiplier=0,
                   allow_small_or_imprecise_dtypes=True).then_inc(const_ready, 1)
            g.iota(iota_run[:, :], pattern=[[1, RUNS * P]], base=0, channel_multiplier=0,
                   allow_small_or_imprecise_dtypes=True).then_inc(const_ready, 1)
            g.iota(iota_b[:, :], pattern=[[1, NB]], base=0, channel_multiplier=0,
                   allow_small_or_imprecise_dtypes=True).then_inc(const_ready, 1)
            g.iota(iota_w[:, :], pattern=[[1, BLK]], base=0, channel_multiplier=0,
                   allow_small_or_imprecise_dtypes=True).then_inc(const_ready, 1)
            g.iota(iota_pk[:, :], pattern=[[1, RUNS]], base=0, channel_multiplier=RUNS,
                   allow_small_or_imprecise_dtypes=True).then_inc(const_ready, 1)
            g.iota(iota_t[:, :], pattern=[[1, TAB // P]], base=0, channel_multiplier=TAB // P,
                   allow_small_or_imprecise_dtypes=True).then_inc(const_ready, 1)

            pool.sem_inc(hist_done, HISTCREDIT)
            pool.sem_inc(steps_used, STEPCREDIT)
            pool.sem_inc(x0_kept, 1)
            pool.sem_inc(part_ready, READYCREDIT)
            pool.sem_inc(part_added, ADDCREDIT)

            def taken_up():
                pool.sem_inc(pool_groups, 1)

            with pool.Fori(0, XOUT) as j:
                for q in range(XR):
                    pool.wait_ge(x0_idx, j * XR + (q + 1))
                    taken_up()
                    for k in range(q * XG, q * XG + XG):
                        pool.indirect_dma_start(
                            out=xg[0:HALF, k, :], out_offset=None, in_=emb,
                            in_offset=bass.IndirectOffsetOnAxis(ap=idx[0:HALF, k:k + 1], axis=0),
                        ).then_inc(x0_got[q], DMA)

            pool.wait_ge(zero_filled, 4 * DMA)

            def scatter(i, q, first):
                pool.wait_ge(stage_ready, i * 2 + (q + 1))
                if not (first and q == 0):
                    pool.wait_ge(scattered[1 - q], i * (RUNS * DMA) + q * (RUNS * DMA))
                taken_up()
                for k in range(RUNS):
                    pool.indirect_dma_start(
                        out=sorted_edges,
                        out_offset=bass.IndirectOffsetOnAxis(ap=run_idx[:, q, k:k + 1], axis=0),
                        in_=stage[:, q, k * RUN:(k + 1) * RUN, :].rearrange("p c f -> p (c f)"), in_offset=None,
                        compute_op=ALU.add,
                    ).then_inc(scattered[q], DMA)

            def move_vals(i, q):
                n = i * 2 + q
                pool.wait_ge(in_slot_ready, n + 1)
                g.tensor_tensor(moved[q][:, :, 1, :], in_slot[q],
                                raw_val[:, bass.ds(n * LANES, LANES)][:, :, None].to_broadcast([P, LANES, SLOTS]),
                                ALU.mult).then_inc(vals_moved, 1)

            move_vals(0, 0)
            move_vals(0, 1)
            scatter(0, 0, True)
            move_vals(1, 0)
            scatter(0, 1, True)
            with pool.Fori(1, PAIRS) as i:
                move_vals(i, 1)
                scatter(i, 0, False)
                move_vals(i + 1, 0)
                scatter(i, 1, False)
            scatter(PAIRS, 0, False)

            for q in range(XR):
                pool.wait_ge(x0_stored[q], XOUT * 2 * DMA)
            with pool.Fori(0, LAYERS) as la:
                with pool.Fori(0, STEPS) as i:
                    for gr in range(RING):
                        pool.wait_ge(idx_ready, la * GROUPS + i * RING + (gr + 1))
                        taken_up()
                        for k in range(gr * GRP, gr * GRP + GRP):
                            pool.indirect_dma_start(
                                out=xg[:, k, :], out_offset=None, in_=x_now,
                                in_offset=bass.IndirectOffsetOnAxis(ap=idx[:, k:k + 1], axis=0),
                            ).then_inc(gathered[gr], DMA)
                pool.wait_ge(part_added, ADDCREDIT + la * TILES + TILES)
                pool.wait_ge(part_ready, READYCREDIT + la * GROUPS + GROUPS)


                def product(i, k, b):
                    if after(b, 2):
                        pool.wait_ge(z_ready, la * NB + i * DUNROLL + (k - 1))
                    g.tensor_tensor(prodT[k % 2], hT[:, columns(i, k)], xT[:, columns(i, k)], ALU.mult).then_inc(prod_ready, 1)

                all_blocks(pool, product)
                for r in range(XNEW):
                    pool.wait_ge(stored[r], la * STORES + STORES)

        @block.sync
        def _(sp):
            for k, src in enumerate((row, col, vals)):
                dst = (raw_row, raw_col, raw_val)[k]
                sp.dma_start(dst, src.rearrange("(p c) -> p c", p=P)).then_inc(edges_in, DMA)
            sp.dma_start(ids_c[:, :], ids.rearrange("(c r) -> c r", r=HALF)).then_inc(ids_in, DMA)
            for k, w in enumerate(weights):
                sp.dma_start(w_raw[:, k, :], w).then_inc(w_in, DMA)
            for k, b in enumerate(biases):
                sp.dma_start(bias[:, 1 + k % 2, k // 2:k // 2 + 1], b.rearrange("(d a) -> d a", a=1)).then_inc(w_in, DMA)
            sp.wait_ge(zeros_ready, 1)
            fill = sorted_edges.rearrange("(p t) c -> p (t c)", p=P)
            for k in range(4):
                sp.dma_start(fill[:, k * ZW:(k + 1) * ZW], zeros[:, 0:ZW]).then_inc(zero_filled, DMA)

            x0_out = out.rearrange("(n k r) f -> n r k f", k=XG, r=HALF)
            x0_now = x_now.rearrange("(n k r) f -> n r k f", k=XG, r=HALF)
            with sp.Fori(0, XOUT) as j:
                for q in range(XR):
                    sp.wait_ge(x0_got[q], j * (XG * DMA) + XG * DMA)
                    sp.dma_start(x0_out[bass.ds(j * XR + q, 1), :, :, 0:D].rearrange("a r k f -> (a r) k f"),
                                 xg[0:HALF, q * XG:q * XG + XG, :]).then_inc(x0_stored[q], DMA)
                    sp.dma_start(x0_now[bass.ds(j * XR + q, 1), :, :, :].rearrange("a r k f -> (a r) k f"),
                                 xg[0:HALF, q * XG:q * XG + XG, :]).then_inc(x0_stored[q], DMA)

            sp.wait_ge(places_ready, 1)
            for k in range(2):
                sp.dma_start(chunk_places[k, :].rearrange("(c b) -> c b", b=NB), places_hl[:, k, :]).then_inc(places_stored, DMA)
            sp.wait_ge(places_stored, 2 * DMA)
            sp.dma_start(places, chunk_places).then_inc(places_in, DMA)
            sp.wait_ge(tab_ready, 1)
            sp.dma_start(tile_offsets, tab_i[:, :]).then_inc(tab_stored, DMA)
            sp.wait_ge(tab_stored, DMA)
            sp.wait_ge(scattered[0], (PAIRS + 1) * RUNS * DMA)
            sp.wait_ge(scattered[1], PAIRS * RUNS * DMA)
            sp.dma_start(unsorted.rearrange("p g l f -> p (g l f)"),
                         sorted_edges[0:DUMP, :].rearrange("(p t) c -> p (t c)", p=P)).then_inc(recs_in, DMA)
            sp.dma_start(table, tile_offsets.rearrange("p t -> (p t)").rearrange("(a t) -> a t", a=1)).then_inc(tab_in, DMA)

            new_out = out.rearrange("(n h r) (l d) -> n l r h d", h=2, r=HALF, d=D)
            new_now = x_now.rearrange("(n h r) d -> n r h d", h=2, r=HALF)
            with sp.Fori(0, LAYERS) as la:
                with sp.Fori(0, NB // XNEW) as j:
                    for r in range(XNEW):
                        sp.wait_ge(rows_ready, la * NB + j * XNEW + (r + 1))
                        sp.dma_start(
                            new_out[bass.ds(j * XNEW + r, 1), bass.ds(la + 1, 1), :, :, :].rearrange("a b r h d -> (a b r) h d"),
                            x_new[r]).then_inc(stored[r], DMA)
                        sp.dma_start(new_now[bass.ds(j * XNEW + r, 1), :, :, :].rearrange("a r h d -> (a r) h d"),
                                     x_new[r]).then_inc(stored[r], DMA)
            for r in range(XNEW):
                sp.wait_ge(stored[r], LAYERS * STORES)

        @block.scalar
        def _(act):
            s = nc.scalar
            act.wait_ge(const_ready, CONSTS)
            act.wait_ge(ids_ready, 1)

            def x0_index(col0, q):
                s.activation(idx[0:HALF, q * XG:q * XG + XG], ids_t[:, col0], ACT.Copy).then_inc(x0_idx, 1)

            def x0_keep(n, count):
                act.wait_ge(x0_turned, count)
                s.activation(xT[:, bass.ds(n * (XG * HALF), XG * HALF)], ps[:, 3, 0:XG * HALF], ACT.Copy).then_inc(x0_kept, 1)

            for n in range(XR - 1):
                x0_index(slice(n * XG, n * XG + XG), n)
            x0_keep(0, 1)
            x0_index(slice((XR - 1) * XG, XR * XG), XR - 1)
            with act.Fori(0, XOUT - 1) as j:
                for q in range(XR):
                    x0_keep(j * XR + (q + 1), j * XR + (q + 2))
                    act.wait_ge(x0_stored[q], j * (2 * DMA) + 2 * DMA)
                    x0_index(bass.ds(j * (XR * XG) + (XR + q) * XG, XG), q)
            for n in range(XGROUPS - XR + 1, XGROUPS):
                x0_keep(n, n + 1)

            act.wait_ge(run_tab_ready, 1)

            def stage_chunk(i, q, first):
                if not first:
                    act.wait_ge(scattered[q], i * (RUNS * DMA))
                s.activation(run_idx[:, q, :], run_tab[:, :, bass.ds(i * 2 + q, 1)].rearrange("p k a -> p (k a)"), ACT.Copy)
                act.wait_ge(ordered, i * 2 + (q + 1))
                s.activation(stage[:, q, :, :], ps[:, 6 + q, 0:2 * SLOTS].rearrange("p (f c) -> p c f", f=2),
                             ACT.Copy).then_inc(stage_ready, 1)

            def find_parts(i, q, first):
                n = i * 2 + q
                act.wait_ge(part_found, n + 1)
                if not first:
                    act.wait_ge(ordered, n - 1)
                act.sem_inc(act_copies, 1)
                for k in range(ACTL):
                    last = s.activation(to_part[q][:, k, :], iota_p[:, :], ACT.Abs, bias=place[:, q, 2, k:k + 1], scale=-1.0)
                last.then_inc(parts_link, 1)
                act.wait_ge(parts_link, n + 1)
                s.activation(to_part[q][:, 0:ACTL, :], to_part[q][:, 0:ACTL, :], ACT.Relu, bias=1.0,
                             scale=-1.0).then_inc(parts_ready, 1)

            find_parts(0, 0, True)
            find_parts(0, 1, True)
            stage_chunk(0, 0, True)
            find_parts(1, 0, False)
            stage_chunk(0, 1, True)
            with act.Fori(1, PAIRS) as i:
                find_parts(i, 1, False)
                stage_chunk(i, 0, False)
                find_parts(i + 1, 0, False)
                stage_chunk(i, 1, False)
            stage_chunk(PAIRS, 0, False)

            keep_turned(act, s.activation, 1, ACT.Copy)
            act.wait_ge(col_ready, 1)
            with act.Fori(0, LAYERS) as la:
                with act.Fori(0, STEPS) as i:
                    for gr in range(RING):
                        act.wait_ge(part_ready, la * GROUPS + i * RING + (gr + 1))
                        s.activation(idx[:, gr * GRP:gr * GRP + GRP], recs[:, 0, bass.ds(i * STEP + gr * GRP, GRP)],
                                     ACT.Copy).then_inc(idx_ready, 1)


                def keep_new(i, k):
                    act.wait_ge(new_ready, la * NB + i * DUNROLL + (k + 1))
                    act.sem_inc(act_copies, 1)
                    s.activation(xT[:, columns(i, k)], newT[k % 2], ACT.Copy).then_inc(xT_ready, 1)

                def bias_step(i, k, b):
                    n = la * NB + i * DUNROLL + k
                    act.wait_ge(z_ready, n + 1)
                    if after(b, 2):
                        act.wait_ge(new_ready, n - 1)
                    if b == 0:
                        act.wait_ge(zconst_ready, la + 1)
                    s.activation(biased[k % 2], zps[k % 2], ACT.Identity, bias=b_now[:, 0:1]).then_inc(biased_ready, 1)
                    s.activation(hT[:, columns(i, k)], zero_blk, ACT.Copy).then_inc(blk_zeroed, 1)
                    if after(b, 1):
                        keep_new(*block_before(i, k))

                all_blocks(act, bias_step)
                keep_new(*last_block)

        @block.tensor
        def _(pe):
            t = nc.tensor
            pe.wait_ge(const_ready, CONSTS)
            pe.wait_ge(w_in, 4 * LAYERS * DMA)
            for k in range(2 * LAYERS):
                last = t.transpose(ps[:, 5 + k // 4, (k % 4) * D:(k % 4 + 1) * D], w_raw[:, k, :], ident[:, :])
            last.then_inc(w_turned, 1)
            pe.wait_ge(ids_float, 1)
            t.transpose(ps[0:HALF, 7, 0:N // HALF], ids_f[:, :], ident[0:N // HALF, 0:N // HALF]).then_inc(ids_turned, 1)

            def hist(b, r):
                pe.wait_ge(onehot_ready, b + 1)
                for k in range(LANES):
                    last = t.matmul(acc[:, bass.ds(b, 1)], in_block[r].rearrange("p (c l) -> p l c", l=LANES)[:, k, :],
                                    ones_b[:, 0:1], start=k == 0, stop=k == LANES - 1)
                last.then_inc(hist_done, 1)

            with pe.Fori(0, XOUT) as j:
                for q in range(XR):
                    for r in range(q * HX, (q + 1) * HX):
                        hist(j * (XR * HX) + r, r % SR)
                    pe.wait_ge(x0_got[q], j * (XG * DMA) + XG * DMA)
                    pe.wait_ge(x0_kept, j * XR + (q + 1))
                    for k in range(XG):
                        last = t.transpose(ps[:, 3, k * HALF:(k + 1) * HALF], xg[0:HALF, q * XG + k, :], ident[0:HALF, 0:HALF])
                    last.then_inc(x0_turned, 1)

            pe.wait_ge(counts_ready, 1)
            t.matmul(ps[:, 4, 0:NB], ones_f[0:CHUNKS, :], small[0:CHUNKS, 0, 0:NB], start=True, stop=True)
            t.matmul(ps[0:CHUNKS, 5, 0:NB], before_f[0:CHUNKS, 0:CHUNKS], small[0:CHUNKS, 0, 0:NB],
                     start=True, stop=True).then_inc(sums_ready, 1)
            pe.wait_ge(ids_ready, 1)
            pe.wait_ge(zeros_ready, 1)
            t.matmul(ps[:, 7, 0:RUNS * CHUNKS], ones_b[0:1, :], zeros.bitcast(BF16)[0:1, 0:RUNS * CHUNKS],
                     start=True, stop=True)
            with pe.Fori(0, (NB + 1) // STR) as j:
                for r in range(STR):
                    pe.wait_ge(steps_ready, j * STR + (r + 1))
                    for k in range(RUNS):
                        for h in range(2):
                            last = t.matmul(ps[:, 7, k * CHUNKS:(k + 1) * CHUNKS],
                                            run_step[r].rearrange("c (p k) -> c k p", k=RUNS)[:, k, :],
                                            run_diag[r][:, h, :], start=False, stop=True, skip_group_check=True)
                    last.then_inc(steps_used, 1)
            pe.wait_ge(places_in, DMA)
            pe.wait_ge(x0_kept, XGROUPS + 1)

            def rank(i, q, first):
                n = i * 2 + q
                pe.wait_ge(onehot2_ready, n + 1)
                if not first:
                    pe.wait_ge(rank_read, n - 1)
                mm = lambda a, l0, l1, lhs, rhs, **kw: t.matmul(
                    ps[:, 3 * q + a, (l0 - a * BANKL) * NB:(l1 - a * BANKL) * NB], lhs, rhs, skip_group_check=True, **kw)
                spread = lambda src, k: src[:, None, :].to_broadcast([src.shape[0], k, NB])
                for a, lanes in LANE_BANKS:
                    l0, l1 = a * BANKL, a * BANKL + lanes
                    mm(a, l0, l1, ones_b[0:2, :], spread(places[:, bass.ds(n * NB, NB)], lanes), start=True, stop=False)
                    mm(a, l0, l1, before[:, :], oh[:, q, l0:l1, :].rearrange("p l b -> p (l b)"), start=False, stop=False)
                    for k in range(l1 // SUMMED - 1):
                        to = max(l0, (k + 1) * SUMMED)
                        mm(a, to, l1, ones_b[:, :], spread(sums[:, q, k, :], l1 - to), start=False, stop=False)
                    for src in range(l0, l1 - 1):
                        end = (src // SUMMED + 1) * SUMMED
                        if src + 1 < end:
                            last = mm(a, src + 1, end, ones_b[:, :], spread(oh[:, q, src, :], end - src - 1),
                                      start=False, stop=src == l1 - 2)
                last.then_inc(rank_ready, 1)

            def order(i, q, first):
                n = i * 2 + q
                pe.wait_ge(moved_ready, n + 1)
                pe.wait_ge(vals_moved, n + 1)
                pe.wait_ge(parts_ready, n + 1)
                if not first:
                    pe.wait_ge(stage_ready, n - 1)
                for k in range(LANES):
                    last = t.matmul(ps[:, 6 + q, 0:2 * SLOTS], to_part[q][:, k, :],
                                    moved[q][:, k, :, :].rearrange("p f c -> p (f c)"), start=k == 0, stop=k == LANES - 1)
                last.then_inc(ordered, 1)

            for q in range(2):
                rank(0, q, True)
            for q in range(2):
                rank(1, q, False)
                order(0, q, True)
            with pe.Fori(1, PAIRS - 1) as i:
                for q in range(2):
                    rank(i + 1, q, False)
                    order(i, q, False)
            rank(PAIRS, 0, False)
            for q in range(2):
                order(PAIRS - 1, q, False)
            order(PAIRS, 0, False)

            pe.wait_ge(recs_in, DMA)
            for m, (f, g0, g1) in enumerate(TURNS):
                if m >= 8:
                    pe.wait_ge(turned_kept[f], (m - 8) // 2 + 1)
                for k in range(g0, g1):
                    last = t.transpose(ps[:, m % 8, (k - g0) * P:(k - g0 + 1) * P], unsorted[:, k, :, f], ident[:, :])
                last.then_inc(turned, 1)

            pe.wait_ge(w_ready, 1)
            with pe.Fori(0, LAYERS) as la:
                with pe.Fori(0, STEPS) as i:
                    for gr in range(RING):
                        n = la * GROUPS + i * RING
                        pe.wait_ge(gathered[gr], la * (STEPS * GRP * DMA) + i * (GRP * DMA) + GRP * DMA)
                        pe.wait_ge(sel_ready, n + (gr + 1))
                        pe.wait_ge(part_added, la * TILES + i * STEP + (gr + 1) * GRP)
                        for k in range(GRP):
                            last = t.matmul(part[(gr % 2) * GRP + k], xg[:, gr * GRP + k, :],
                                            sel[:, (gr % 2) * GRP + k, :], start=True, stop=True)
                        last.then_inc(part_ready, 1)


                def turn(i, k):
                    for h in range(2):
                        last = t.transpose(tps[k % 2][:, h, :], newT[k % 2][:, h * HALF:(h + 1) * HALF], ident[:, :])
                    last.then_inc(new_turned, 1)

                pe.wait_ge(w_now_ready, la + 1)

                def dense(i, k, b):
                    n = la * NB + i * DUNROLL + k
                    pe.wait_ge(sum_ready, n + 1)
                    pe.wait_ge(prod_ready, n + 1)
                    if after(b, 2):
                        pe.wait_ge(biased_ready, n - 1)
                    t.matmul(zps[k % 2], w_now[:, 0, :], sumT[k % 2], start=True, stop=False)
                    t.matmul(zps[k % 2], w_now[:, 1, :], prodT[k % 2], start=False, stop=True).then_inc(z_ready, 1)
                    if after(b, 1):
                        pe.wait_ge(new_ready, n)
                        if after(b, 3):
                            pe.wait_ge(rows_ready, n - 2)
                        turn(*block_before(i, k))

                all_blocks(pe, dense)
                pe.wait_ge(new_ready, la * NB + NB)
                pe.wait_ge(rows_ready, la * NB + (NB - 2))
                turn(*last_block)

        @block.vector
        def _(dve):
            v = nc.vector
            links = [0]

            def link(ins):
                links[0] += 1
                ins.then_inc(dve_link, 1)
                dve.wait_ge(dve_link, links[0])

            v.memset(zeros, 0.0).then_inc(zeros_ready, 1)
            dve.wait_ge(ids_in, DMA)
            v.tensor_copy(ids_f[:, :], ids_c[:, :]).then_inc(ids_float, 1)
            dve.wait_ge(ids_turned, 1)
            v.tensor_copy(ids_t[:, :], ps[0:HALF, 7, 0:N // HALF]).then_inc(ids_ready, 1)

            dve.wait_ge(edges_in, 3 * DMA)
            exact = hT[:, OP0:OP0 + COLS]
            link(v.tensor_scalar(exact, raw_row, -(BLK - 1) / 2, 1.0 / BLK, ALU.add, ALU.mult))
            link(v.tensor_scalar(block_of, exact, ROUND, -ROUND, ALU.add, ALU.add))
            link(v.scalar_tensor_tensor(packed, block_of, -float(BLK), raw_row, ALU.mult, ALU.add))
            v.scalar_tensor_tensor(packed, raw_col, PACK, packed, ALU.mult, ALU.add).then_inc(packed_ready, 1)

            dve.wait_ge(const_ready, CONSTS)

            with dve.Fori(0, NB // SR) as j:
                for r in range(SR):
                    dve.wait_ge(hist_done, j * SR + (r + 1))
                    v.tensor_scalar(in_block[r], block_of, iota_b[:, bass.ds(j * SR + r, 1)], None,
                                    ALU.is_equal).then_inc(onehot_ready, 1)

            def one_hot(it, r):
                return v.tensor_tensor(oh[:, r, :, :],
                                       block_of[:, bass.ds(it * LANES, LANES)][:, :, None].to_broadcast([P, LANES, NB]),
                                       iota_b[:, None, :].to_broadcast([P, LANES, NB]), ALU.is_equal)

            dve.wait_ge(w_turned, 1)
            wf = w_sb[:, :, :, :].rearrange("p l k d -> p (l k d)")
            v.tensor_copy(ident_b[:, :], ident[:, :])
            v.tensor_copy(wf[:, 0:4 * D], ps[:, 5, 0:4 * D])
            v.tensor_copy(wf[:, 4 * D:6 * D], ps[:, 6, 0:2 * D])
            v.tensor_tensor(bias[:, 0, :], bias[:, 1, :], bias[:, 2, :], ALU.add).then_inc(w_ready, 1)

            names = "count sum_ before_ n_tiles end_tile ones cursor run0 phase n_runs end_run start_run at shift by_high by_low".split()
            of = {name: small[0:CHUNKS, k, 0:NB] for k, name in enumerate(names)}
            whole = {name: small[:, k, 0:NB] for k, name in enumerate(names)}
            dve.wait_ge(hist_done, NB + HISTCREDIT)
            v.memset(whole["ones"], 1.0)
            v.tensor_copy(of["count"], acc).then_inc(counts_ready, 1)
            dve.wait_ge(sums_ready, 1)
            link(v.tensor_scalar(whole["sum_"], ps[:, 4, 0:NB], (P - 1) / 2, 1.0 / P, ALU.add, ALU.mult))
            link(v.tensor_scalar(whole["n_tiles"], whole["sum_"], ROUND, -ROUND, ALU.add, ALU.add))
            link(v.tensor_tensor_scan(whole["end_tile"], whole["ones"], whole["n_tiles"], 0.0, ALU.mult, ALU.add))
            link(v.tensor_tensor(whole["at"], whole["end_tile"], whole["n_tiles"], ALU.subtract))
            link(v.scalar_tensor_tensor(of["cursor"], of["at"], float(P), ps[0:CHUNKS, 5, 0:NB], ALU.mult, ALU.add))
            link(v.tensor_scalar(of["before_"], of["cursor"], -(RUN - 1) / 2, 1.0 / RUN, ALU.add, ALU.mult))
            link(v.tensor_scalar(of["run0"], of["before_"], ROUND, -ROUND, ALU.add, ALU.add))
            link(v.scalar_tensor_tensor(of["phase"], of["run0"], -float(RUN), of["cursor"], ALU.mult, ALU.add))
            link(v.tensor_tensor(of["at"], of["phase"], of["count"], ALU.add))
            link(v.tensor_scalar(of["before_"], of["at"], (RUN - 1) / 2, 1.0 / RUN, ALU.add, ALU.mult))
            link(v.tensor_scalar(of["n_runs"], of["before_"], ROUND, -ROUND, ALU.add, ALU.add))
            link(v.tensor_tensor_scan(of["end_run"], of["ones"], of["n_runs"], 0.0, ALU.mult, ALU.add))
            link(v.tensor_tensor(of["start_run"], of["end_run"], of["n_runs"], ALU.subtract))
            link(v.scalar_tensor_tensor(of["at"], of["start_run"], float(RUN), of["phase"], ALU.mult, ALU.add))
            link(v.tensor_scalar(of["before_"], of["at"], -(QHI - 1) / 2, 1.0 / QHI, ALU.add, ALU.mult))
            link(v.tensor_scalar(of["cursor"], of["before_"], ROUND, -ROUND, ALU.add, ALU.add))
            v.tensor_scalar(places_hl[:, 0, :], of["cursor"], QHI, None, ALU.mult)
            v.scalar_tensor_tensor(places_hl[:, 1, :], of["cursor"], -QHI, of["at"],
                                   ALU.mult, ALU.add).then_inc(places_ready, 1)
            link(v.tensor_tensor(of["shift"], of["run0"], of["start_run"], ALU.subtract))
            step_at = small[0:CHUNKS, names.index("start_run"), :]
            step_by = small[0:CHUNKS, names.index("sum_"), :]
            v.tensor_copy(step_at[:, NB:NB + 1], of["end_run"][:, NB - 1:NB])
            v.tensor_copy(step_by[:, 0:1], of["shift"][:, 0:1])
            v.tensor_tensor(step_by[:, 1:NB], of["shift"][:, 1:NB], of["shift"][:, 0:NB - 1], ALU.subtract)
            link(v.tensor_scalar(step_by[:, NB:NB + 1], of["shift"][:, NB - 1:NB], -1.0, float(DUMP), ALU.mult, ALU.add))
            high = small[0:CHUNKS, names.index("by_high"), :]
            low = small[0:CHUNKS, names.index("by_low"), :]
            link(v.tensor_scalar(low, step_by, -(PACK - 1) / 2, 1.0 / PACK, ALU.add, ALU.mult))
            link(v.tensor_scalar(high, low, ROUND, -ROUND, ALU.add, ALU.add))
            link(v.tensor_scalar(high, high, PACK, None, ALU.mult))
            link(v.tensor_tensor(low, step_by, high, ALU.subtract))
            with dve.Fori(0, (NB + 1) // STR) as j:
                for r in range(STR):
                    at = bass.ds(j * STR + r, 1)
                    dve.wait_ge(steps_used, j * STR + (r + 1))
                    v.tensor_scalar(run_step[r], iota_run[0:CHUNKS, :], step_at[:, at], None, ALU.is_ge)
                    for h, height in enumerate((high, low)):
                        last = v.tensor_scalar(run_diag[r][:, h, :], ident_b[0:CHUNKS, 0:CHUNKS], height[:, at], None, ALU.mult)
                    last.then_inc(steps_ready, 1)
            big = ranked[:, :].rearrange("p (t b) -> p t b", b=NB)
            link(v.tensor_tensor(big, iota_t[:, :, None].to_broadcast([P, TABW, NB]),
                                 whole["end_tile"][:, None, :].to_broadcast([P, TABW, NB]), ALU.is_ge))
            link(v.tensor_reduce(tab_f[:, :], big, AX.X, ALU.add))
            v.tensor_scalar(tab_i[:, :], tab_f[:, :], float(NB - 1), float(BLK), ALU.min, ALU.mult).then_inc(tab_ready, 1)
            dve.wait_ge(steps_used, NB + 1 + STEPCREDIT)
            v.tensor_tensor(run_tab[:, :, :], ps[:, 7, 0:RUNS * CHUNKS].rearrange("p (k c) -> p k c", k=RUNS),
                            iota_pk[:, :, None].to_broadcast([P, RUNS, CHUNKS]), ALU.add).then_inc(run_tab_ready, 1)

            def one_hot_sums(n, q):
                dve.wait_ge(sum_link, n + 1)
                with nc.allow_low_precision(reason="counts up to SUMMED are exact"):
                    v.tensor_reduce(sums[:, q, :, :],
                                    oh[:, q, 0:LANES - SUMMED, :].rearrange("p (g l) b -> p g b l", l=SUMMED),
                                    AX.X, ALU.add).then_inc(onehot2_ready, 1)

            def chunk(i, q, first, more):
                n = i * 2 + q
                dve.wait_ge(rank_ready, n + 1)
                v.tensor_tensor(ranked[:, 0:2 * BANKL * NB].rearrange("p (a x) -> p a x", a=2),
                                ps[:, 3 * q:3 * q + 2, 0:BANKL * NB],
                                oh[:, q, 0:2 * BANKL, :].rearrange("p (a l) b -> p a (l b)", a=2), ALU.mult)
                v.tensor_tensor(ranked[:, 2 * BANKL * NB:OHW], ps[:, 3 * q + 2, 0:(LANES - 2 * BANKL) * NB],
                                oh[:, q, 2 * BANKL:LANES, :].rearrange("p l b -> p (l b)"), ALU.mult).then_inc(rank_read, 1)
                dve.wait_ge(rank_read, n + 1)
                if not first:
                    dve.wait_ge(parts_ready, n - 1)
                at, raised, part_of, slot = [place[:, q, k, :] for k in range(4)]
                v.tensor_reduce(at, ranked[:, :].rearrange("p (l b) -> p l b", b=NB), AX.X, ALU.add).then_inc(at_link, 1)
                if more:
                    one_hot(n + 2, q).then_inc(sum_link, 1)
                dve.wait_ge(at_link, n + 1)
                v.tensor_scalar(raised, at, -(SLOTS - 1) / 2, 1.0 / SLOTS, ALU.add, ALU.mult).then_inc(raised_link, 1)
                if more:
                    one_hot_sums(n + 2, q)
                dve.wait_ge(raised_link, n + 1)
                v.tensor_scalar(part_of, raised, ROUND, -ROUND, ALU.add, ALU.add).then_inc(part_found, 1)
                dve.wait_ge(part_found, n + 1)
                v.scalar_tensor_tensor(slot, part_of, -float(SLOTS), at, ALU.mult, ALU.add).then_inc(slot_link, 1)
                if not first:
                    dve.wait_ge(ordered, n - 1)
                dve.wait_ge(slot_link, n + 1)
                v.tensor_tensor(in_slot[q], slot[:, :, None].to_broadcast([P, LANES, SLOTS]),
                                iota_p[:, None, 0:SLOTS].to_broadcast([P, LANES, SLOTS]), ALU.is_equal).then_inc(in_slot_ready, 1)
                v.tensor_tensor(to_part[q][:, ACTL:LANES, :], part_of[:, ACTL:LANES][:, :, None].to_broadcast([P, LANES - ACTL, P]),
                                iota_p[:, None, :].to_broadcast([P, LANES - ACTL, P]), ALU.is_equal)
                dve.wait_ge(in_slot_ready, n + 1)
                v.tensor_tensor(moved[q][:, :, 0, :], in_slot[q],
                                packed[:, bass.ds(n * LANES, LANES)][:, :, None].to_broadcast([P, LANES, SLOTS]),
                                ALU.mult).then_inc(moved_ready, 1)

            dve.wait_ge(zero_filled, 4 * DMA)
            dve.wait_ge(x0_kept, XGROUPS + 1)
            for q in range(XR):
                dve.wait_ge(x0_stored[q], XOUT * 2 * DMA)
            for q in range(2):
                one_hot(q, q).then_inc(sum_link, 1)
                one_hot_sums(q, q)
            for q in range(2):
                chunk(0, q, True, True)
            with dve.Fori(1, PAIRS - 1) as i:
                for q in range(2):
                    chunk(i, q, False, True)
            chunk(PAIRS - 1, 0, False, True)
            chunk(PAIRS - 1, 1, False, False)
            chunk(PAIRS, 0, False, False)

            keep_turned(dve, v.tensor_copy, 0)
            dve.wait_ge(turned_kept[0], len(TURNS) // 2)
            link(v.tensor_scalar(recs[:, 1, :], recs[:, 0, :], -(PACK - 1) / 2, 1.0 / PACK, ALU.add, ALU.mult))
            link(v.tensor_scalar(recs[:, 1, :], recs[:, 1, :], ROUND, -ROUND, ALU.add, ALU.add))
            row_in = hT[:, 0:TAB]
            link(v.scalar_tensor_tensor(row_in, recs[:, 1, :], -PACK, recs[:, 0, :], ALU.mult, ALU.add))
            v.tensor_copy(recs[:, 0, :], recs[:, 1, :]).then_inc(col_ready, 1)
            dve.wait_ge(col_ready, 1)
            link(v.tensor_copy(recs[:, 1, :], row_in))
            dve.wait_ge(turned_kept[1], len(TURNS) // 2)
            link(v.memset(hT[:, :], 0.0))
            dve.wait_ge(tab_in, DMA)
            with dve.Fori(0, LAYERS) as la:
                v.tensor_copy(b_now[:, :], bias[:, 0, bass.ds(la, 1)])
                v.tensor_copy(w_now[:, :, :], w_sb[:, bass.ds(la, 1), :, :].rearrange("p a k d -> p (a k) d")).then_inc(w_now_ready, 1)

                def select(t0, gr, k):
                    slot = (gr % 2) * GRP + k
                    at = bass.ds(t0 + (gr * GRP + k), 1)
                    return v.tensor_scalar(sel[:, slot, :], iota_w[:, :], recs[:, 1, at], recs[:, 2, at],
                                           ALU.is_equal, ALU.mult)

                def step(t0, i, last_step):
                    for gr in range(RING):
                        _, offs = nc.values_load_multi_w_load_instructions(
                            table[0:1, bass.ds(t0 + gr * GRP, GRP)], engines=[mybir.EngineType.DVE],
                            min_val=0, max_val=N - BLK, skip_runtime_bounds_check_because="the table holds offsets of blocks")
                        dve.wait_ge(part_ready, la * GROUPS + i * RING + (READYCREDIT + gr + 1))
                        for k in range(GRP):
                            dve.wait_ge(part_added, la * TILES + i * STEP + (ADDCREDIT + gr * GRP + k))
                            blk = hT[:, bass.ds(offs[k], BLK)]
                            v.tensor_tensor(blk, blk, part[(gr % 2) * GRP + k], ALU.add).then_inc(part_added, 1)
                            if not (last_step and gr >= RING - 2):
                                built = select(t0, gr + 2, k)
                                if k == GRP - 1:
                                    built.then_inc(sel_ready, 1)

                for gr in range(2):
                    for k in range(GRP):
                        built = select(0, gr, k)
                    built.then_inc(sel_ready, 1)
                with dve.Fori(0, STEPS - 1) as i:
                    step(i * STEP, i, False)
                step((STEPS - 1) * STEP, STEPS - 1, True)

                dve.wait_ge(part_added, la * TILES + (ADDCREDIT + TILES))
                v.memset(zero_blk, 0.0).then_inc(zconst_ready, 1)


                def make_sum(i, k, b):
                    if after(b, 2):
                        dve.wait_ge(z_ready, la * NB + i * DUNROLL + (k - 1))
                    v.tensor_tensor(sumT[k % 2], hT[:, columns(i, k)], xT[:, columns(i, k)], ALU.add).then_inc(sum_ready, 1)

                def keep_rows(i, k, b):
                    dve.wait_ge(new_turned, la * NB + i * DUNROLL + (k + 1))
                    if after(b, XNEW):
                        dve.wait_ge(stored[k % XNEW], la * STORES + i * (DUNROLL // XNEW * 2 * DMA) + k // XNEW * 2 * DMA)
                    v.tensor_copy(x_new[k % XNEW], tps[k % 2]).then_inc(rows_ready, 1)

                def leaky(i, k, b):
                    n = la * NB + i * DUNROLL + k
                    if b != NB - 1:
                        nxt = None if b is None else b + 1
                        make_sum(i, k + 1, nxt) if k + 1 < DUNROLL else make_sum(i + 1, 0, nxt)
                    dve.wait_ge(biased_ready, n + 1)
                    if after(b, 2):
                        dve.wait_ge(new_turned, n - 1)
                        dve.wait_ge(xT_ready, n - 1)
                    v.scalar_tensor_tensor(newT[k % 2], biased[k % 2], SLOPE, biased[k % 2], ALU.mult, ALU.max).then_inc(new_ready, 1)
                    if after(b, 1):
                        keep_rows(*block_before(i, k), None if b is None else b - 1)

                make_sum(0, 0, 0)
                all_blocks(dve, leaky)
                keep_rows(*last_block, NB - 1)
                dve.wait_ge(blk_zeroed, la * NB + NB)
                dve.wait_ge(xT_ready, la * NB + NB)


_INS = ["r_x_ids", "L0_rec_row", "L0_rec_col", "L0_rec_vals", "L0_rec_emb"]
_LAYERS = [("L0_rec_W%d_%d" % (la, k), "L0_rec_b%d_%d" % (la, k)) for la in (1, 2, 3) for k in (1, 2)]


def kernel(**inputs):
    import numpy as np
    import concourse.bacc as bacc
    from concourse.bass_utils import run_bass_kernel_spmd

    nc = bacc.Bacc("TRN2", target_bir_lowering=False, num_devices=1)
    arrays, aps = {}, {}
    for name in _INS + [n for pair in _LAYERS for n in pair]:
        a = np.ascontiguousarray(inputs[name])
        arrays["in_" + name] = a
        aps[name] = nc.dram_tensor("in_" + name, a.shape, mybir.dt.from_np(a.dtype), kind="ExternalInput").ap()
    out = nc.dram_tensor("out_x", (N, D * (LAYERS + 1)), F32, kind="ExternalOutput").ap()
    graph_layers(nc, *[aps[n] for n in _INS], [aps[w] for w, _ in _LAYERS], [aps[b] for _, b in _LAYERS], out)
    r = run_bass_kernel_spmd(nc, [arrays], core_ids=[0])
    return r.results[0]["out_x"]
```
